# Optimizing a Trainium2 kernel written in Bass

```python
import numpy as np
import jax
import jax.numpy as jnp

def _softmax(x, axis=-1):
    return jax.nn.softmax(x, axis=axis)

def _gelu(x):
    return jax.nn.gelu(x, approximate=True)

def _silu(x):
    return jax.nn.silu(x)

def _sigmoid(x):
    return jax.nn.sigmoid(x)

def _layernorm(x, axis=-1, eps=1e-05):
    m = jnp.mean(x, axis=axis, keepdims=True)
    v = jnp.var(x, axis=axis, keepdims=True)
    return (x - m) / jnp.sqrt(v + eps)

def _scatter_add(tgt, idx, src, axis=0):
    return tgt.at[idx].add(src)

def _segment_sum(src, seg, n):
    return jax.ops.segment_sum(src, seg, n)
kernel_name = 'mk_adj_resnorm_d2_adj_r2_b5f724'

def setup_inputs(seed: int=0):
    np.random.seed(seed)
    _w = jnp.asarray

    def _rec_inputs():
        import jax
        import jax.numpy as jnp
        _gk = jax.random.key(seed)
        x = -0.0005207 + 1.001 * jax.random.normal(jax.random.fold_in(_gk, 1), (64, 128, 256), jnp.float32)
        _a = jax.random.bernoulli(jax.random.fold_in(_gk, 2), 0.0625, (64, 128, 128))
        adj = _a.astype(jnp.int32)
        return (x, adj)
    x, adj = _rec_inputs()

    def _L0_gnn_setup():
        import jax, jax.numpy as jnp
        import numpy as np
        NEG_INF = -1e+30
        NEG_SLOPE = 0.2
        key = jax.random.key(seed)
        k1, k2, k3, k4, k5 = jax.random.split(key, 5)
        B, N, D, H = (2, 1024, 256, 8)
        k = D // H
        return {'x': jax.random.normal(k1, (B, N, D), dtype=jnp.float32), 'A': jax.random.randint(k2, (B, N, N), 0, 2, dtype=jnp.int32), 'W_proj': jax.random.normal(k3, (D, D), dtype=jnp.float32) * (1.0 / np.sqrt(D)), 'W_att': jax.random.normal(k4, (H, 2 * k), dtype=jnp.float32) * (1.0 / np.sqrt(2 * k)), 'b_att': jax.random.normal(k5, (H,), dtype=jnp.float32) * 0.01}
    _L0_gnn_all = _L0_gnn_setup()
    _L0_gnn_in = {k: v for k, v in _L0_gnn_all.items() if k in ('W_proj', 'W_att', 'b_att')}
    del _L0_gnn_all

    def _L1_gnn_setup():
        import jax, jax.numpy as jnp
        import numpy as np
        L = 3
        D = 256
        B, N = (8, 512)
        EPS = 1e-05

        def layernorm(x, gamma, beta):
            mu = jnp.mean(x, axis=-1, keepdims=True)
            var = jnp.var(x, axis=-1, keepdims=True)
            return (x - mu) * jax.lax.rsqrt(var + EPS) * gamma + beta
        key = jax.random.key(seed)
        ks = jax.random.split(key, 12)
        s = 1.0 / np.sqrt(D)
        node_features = jax.random.normal(ks[0], (B, N, D), dtype=jnp.float32)
        adjacency_matrix = jax.random.randint(ks[1], (B, N, N), 0, 2, dtype=jnp.int32)
        return {'node_features': node_features, 'adjacency_matrix': adjacency_matrix, 'attn_w': jax.random.normal(ks[2], (L, 2 * D), dtype=jnp.float32) * (1.0 / np.sqrt(2 * D)), 'attn_b': jax.random.normal(ks[3], (L,), dtype=jnp.float32) * 0.01, 'W1': jax.random.normal(ks[4], (L, D, 4 * D), dtype=jnp.float32) * s, 'b1': jnp.zeros((L, 4 * D), dtype=jnp.float32), 'W2': jax.random.normal(ks[5], (L, 4 * D, D), dtype=jnp.float32) * (1.0 / np.sqrt(4 * D)), 'b2': jnp.zeros((L, D), dtype=jnp.float32), 'g1': jnp.ones((L, D), dtype=jnp.float32), 'beta1': jnp.zeros((L, D), dtype=jnp.float32), 'g2': jnp.ones((L, D), dtype=jnp.float32), 'beta2': jnp.zeros((L, D), dtype=jnp.float32)}
    _L1_gnn_all = _L1_gnn_setup()
    _L1_gnn_in = {k: v for k, v in _L1_gnn_all.items() if k in ('attn_w', 'attn_b', 'W1', 'b1', 'W2', 'b2', 'g1', 'beta1', 'g2', 'beta2')}
    del _L1_gnn_all
    return {'x': x, 'adj': adj, 'L0_gnn_W_proj': _L0_gnn_in['W_proj'], 'L0_gnn_W_att': _L0_gnn_in['W_att'], 'L0_gnn_b_att': _L0_gnn_in['b_att'], 'L1_gnn_attn_w': _L1_gnn_in['attn_w'], 'L1_gnn_attn_b': _L1_gnn_in['attn_b'], 'L1_gnn_W1': _L1_gnn_in['W1'], 'L1_gnn_b1': _L1_gnn_in['b1'], 'L1_gnn_W2': _L1_gnn_in['W2'], 'L1_gnn_b2': _L1_gnn_in['b2'], 'L1_gnn_g1': _L1_gnn_in['g1'], 'L1_gnn_beta1': _L1_gnn_in['beta1'], 'L1_gnn_g2': _L1_gnn_in['g2'], 'L1_gnn_beta2': _L1_gnn_in['beta2']}

def reference(x, adj, L0_gnn_W_proj, L0_gnn_W_att, L0_gnn_b_att, L1_gnn_attn_w, L1_gnn_attn_b, L1_gnn_W1, L1_gnn_b1, L1_gnn_W2, L1_gnn_b2, L1_gnn_g1, L1_gnn_beta1, L1_gnn_g2, L1_gnn_beta2):
    import jax
    import jax.numpy as jnp

    def _L0_gnn_ref(x, A, W_proj, W_att, b_att):
        import jax, jax.numpy as jnp
        import numpy as np
        NEG_INF = -1e+30
        NEG_SLOPE = 0.2
        B, N, _ = x.shape
        H, two_k = W_att.shape
        k = two_k // 2
        xp = jnp.einsum('bnd,do->bno', x, W_proj)
        xh = xp.reshape(B, N, H, k).transpose(0, 2, 1, 3)
        a_src = jnp.einsum('bhnk,hk->bhn', xh, W_att[:, :k])
        a_dst = jnp.einsum('bhnk,hk->bhn', xh, W_att[:, k:])
        scores = a_src[:, :, :, None] + a_dst[:, :, None, :] + b_att[None, :, None, None]
        scores = jax.nn.leaky_relu(scores, negative_slope=NEG_SLOPE)
        mask = (A > 0)[:, None, :, :]
        scores = jnp.where(mask, scores, NEG_INF)
        att = jax.nn.softmax(scores, axis=-1)
        out = jax.nn.relu(jnp.einsum('bhij,bhjk->bhik', att, xh))
        return out.transpose(0, 2, 1, 3).reshape(B, N, H * k)

    def _L1_gnn_ref(node_features, adjacency_matrix, attn_w, attn_b, W1, b1, W2, b2, g1, beta1, g2, beta2):
        import jax, jax.numpy as jnp
        import numpy as np
        L = 3
        D = 256
        B, N = (8, 512)
        EPS = 1e-05

        def layernorm(x, gamma, beta):
            mu = jnp.mean(x, axis=-1, keepdims=True)
            var = jnp.var(x, axis=-1, keepdims=True)
            return (x - mu) * jax.lax.rsqrt(var + EPS) * gamma + beta
        n = adjacency_matrix.shape[-1]
        mask = adjacency_matrix.astype(jnp.float32) + jnp.eye(n, dtype=jnp.float32) > 0
        x = node_features
        d = x.shape[-1]
        for l in range(attn_w.shape[0]):
            si = x @ attn_w[l, :d]
            sj = x @ attn_w[l, d:]
            scores = si[:, :, None] + sj[:, None, :] + attn_b[l]
            scores = jnp.where(scores >= 0, scores, 0.2 * scores)
            scores = jnp.where(mask, scores, -jnp.inf)
            attn = jax.nn.softmax(scores, axis=-1)
            agg = jnp.einsum('bij,bjd->bid', attn, x)
            h = layernorm(x + agg, g1[l], beta1[l])
            ff = jax.nn.gelu(h @ W1[l] + b1[l], approximate=False) @ W2[l] + b2[l]
            x = layernorm(h + ff, g2[l], beta2[l])
        return x
    x = _layernorm(x + _L0_gnn_ref(x, adj, L0_gnn_W_proj, L0_gnn_W_att, L0_gnn_b_att), axis=-1)
    x = _layernorm(x + _L1_gnn_ref(x, adj, L1_gnn_attn_w, L1_gnn_attn_b, L1_gnn_W1, L1_gnn_b1, L1_gnn_W2, L1_gnn_b2, L1_gnn_g1, L1_gnn_beta1, L1_gnn_g2, L1_gnn_beta2), axis=-1)
    return x

_drawn_inputs = setup_inputs


def setup_inputs(seed=0):
    import zlib

    import numpy as np

    out = dict(_drawn_inputs(seed))
    spreads = {'L1_gnn_b1': (0.0, 0.1),
     'L1_gnn_b2': (0.0, 0.1),
     'L1_gnn_g1': (1.0, 0.2),
     'L1_gnn_beta1': (0.0, 0.1),
     'L1_gnn_g2': (1.0, 0.2),
     'L1_gnn_beta2': (0.0, 0.1)}
    factors = {'L0_gnn_b_att': 53.979, 'L1_gnn_attn_b': 64.0}
    for name, (base, spread) in spreads.items():
        noise = np.random.default_rng([zlib.crc32(name.encode()), seed]).standard_normal(out[name].shape)
        drawn = base * np.exp(spread * noise) if base else spread * noise
        out[name] = jnp.asarray(drawn.astype(out[name].dtype))
    for name, factor in factors.items():
        out[name] = (out[name] * factor).astype(out[name].dtype)
    return out
```

```python
from contextlib import ExitStack

import concourse.bass as bass
from concourse import mybir

F32 = mybir.dt.float32
F32R = mybir.dt.float32r
BF16 = mybir.dt.bfloat16
I32 = mybir.dt.int32
ALU = mybir.AluOpType
ACT = mybir.ActivationFunctionType
AX_X = mybir.AxisListType.X

EPS = 1e-5
SLOPE = 0.2
MASKED = -(2.0 ** 100)


def graph_network(nc, x, adj, w_proj, w_att, b_att, attn_w, attn_b, W1, b1, W2, b2,
                  g1, beta1, g2, beta2, out):
    B, N, D = x.shape
    H, K2 = w_att.shape
    KH = K2 // 2
    L = attn_w.shape[0]
    F = W1.shape[2]
    P = N
    G = 4
    S = 2
    TURNS = B // (G * S)
    KD = D // P
    FT = F // P
    NG = G * N
    HW = KH + 2
    XW = D + 2
    assert P == 128 and NG == 512 and H * KH == D and KD == 2

    SLOTS = S * L
    Q = S * H + SLOTS

    def slot(l, s):
        return S * l + s

    with ExitStack() as ctx:
        def sb(name, shape, dt=F32):
            return ctx.enter_context(nc.sbuf_tensor(name, shape, dt))

        def sem(name):
            return ctx.enter_context(nc.semaphore(name))

        w1_hi, w1_lo = (sb(f"w1_{p}", [P, L, KD, F], F32R) for p in ("hi", "lo"))
        w2_hi, w2_lo = (sb(f"w2_{p}", [P, L, FT, D], F32R) for p in ("hi", "lo"))
        PW = D + 2 * H
        wp_hi, wp_lo = (sb(f"wp_{p}", [P, KD, PW], F32R) for p in ("hi", "lo"))
        attw = sb("attw", [P, L, 2 * D])
        gamma1 = sb("gamma1", [P, L, D])
        shift1 = sb("shift1", [P, L, D])
        gamma2 = sb("gamma2", [P, L, D])
        shift2 = sb("shift2", [P, L, D])
        NB, NK = L * FT, L * KD
        cols = sb("cols", [P, NB + 2 * NK])
        bias1 = sb("bias1", [P, NB])
        bias1_part = sb("bias1_part", [P, NB])
        batt = sb("batt", [P, H])
        attb = sb("attb", [P, L])
        ident = sb("ident", [P, P])
        sel = sb("sel", [32 + H, H, P], F32R)
        half_neg = sb("half_neg", [P, G])

        MARKS = 48
        dve_mark = sb("dve_mark", [P, MARKS])
        pool_mark = sb("pool_mark", [P, MARKS])
        dve_marks, pool_marks = (iter([slice(i, i + 1) for i in range(MARKS)]) for _ in range(2))

        x0 = sb("x0", [P, S, G, D])
        xs = sb("xs", [P, S, G, D])
        adj_in = sb("adj_in", [P, G, N], I32)
        edge0 = sb("edge0", [P, S, G, N], BF16)
        edge1 = sb("edge1", [P, S, G, N], BF16)
        xa_hi, xa_lo = (sb(f"xa_{p}", [P, G, XW], F32R) for p in ("hi", "lo"))
        nT_hi, nT_lo = (sb(f"nT_{p}", [P, KD, NG], F32R) for p in ("hi", "lo"))
        G_hi, G_lo = (sb(f"G_{p}", [P, FT * NG], F32R) for p in ("hi", "lo"))
        g_full = sb("g_full", [P, 2, NG])
        u = sb("u", [P, 2, NG])
        w = sb("w", [P, 2, NG])
        row_max = sb("row_max", [P, G])
        neg_z = sb("neg_z", [P, G])
        neg_top = sb("neg_top", [P, 2, G])
        src0 = sb("src0", [P, G, H])
        src1 = sb("src1", [P, G])
        dst1 = sb("dst1", [P, G])
        dst_row = sb("dst_row", [32 + H, P], F32R)
        recip0 = sb("recip0", [P, G, H])
        recip1 = sb("recip1", [P, G])
        NORMS = ("l0", "n1", "n2", "end")
        stats = {k: sb(f"stats_{k}", [P, G, 6]) for k in NORMS}
        meanvar = {k: sb(f"meanvar_{k}", [P, G, 2]) for k in NORMS}
        vareps = {k: sb(f"vareps_{k}", [P, G]) for k in NORMS}
        rstd = {k: sb(f"rstd_{k}", [P, G]) for k in NORMS}

        Gh = G_hi[:, :].rearrange("p (f n) -> p f n", f=FT)
        Gl = G_lo[:, :].rearrange("p (f n) -> p f n", f=FT)
        pT0_hi = [Gh[:, i, :] for i in range(2)]
        pT0_lo = [Gl[:, i, :] for i in range(2)]
        xh_hi = G_hi[:, 2 * NG:2 * NG + G * H * HW].rearrange("p (g h c) -> p g h c", g=G, h=H)
        xh_lo = G_lo[:, 2 * NG:2 * NG + G * H * HW].rearrange("p (g h c) -> p g h c", g=G, h=H)
        dst_rows = G_hi[0:32 + H, 5 * NG:6 * NG]
        stage = [u, w]
        watt_b = xs[:, 0, 0:2, :].rearrange("p a b -> p (a b)")[:, 0:H * K2].rearrange("p (h k) -> p h k", h=H)
        prod = xs[:, 1, 0, :]
        wp_in = x0[:, 0, 0:KD, :]
        wsum = x0[:, 1, 0:KD, 0:2 * H]
        rows_in = xs[0:NB + 2 * NK, 1, 1, 0:P]
        b2_b = xs[:, 0, 0:L, :]

        bank = [ctx.enter_context(nc.psum_tensor(f"bank{i}", [P, 512], F32)) for i in range(8)]
        U0, U1, V0, V1, Z, T, R0, R1 = bank
        up_bank = [U0, U1]
        down_bank = [V0, V1]
        agg_bank = [R0, R1]
        out0_bank = [R0, R1, V0, V1]
        z_bank = [Z, U0]
        pT_bank = [T, U1]

        s_rows = sem("rows_loaded")
        s_consts = sem("consts_loaded")
        s_wp = sem("proj_loaded")
        s_stage = [sem(f"stage_loaded{i}") for i in range(2)]
        s_made = sem("pool_consts_made")
        s_prep = sem("prep_step")
        s_cols_ps = sem("columns_turned")
        s_cols = sem("columns_ready")
        s_bmm = sem("beta_product_done")
        s_hi_done = sem("weight_hi_done")
        s_lo_done = sem("weight_lo_done")
        s_ready = sem("weights_ready")
        s_x = [sem(f"x_loaded{s}") for s in range(S)]
        s_adj = sem("adj_loaded")
        s_adj_used = sem("adj_used")
        s_self = sem("self_edges_added")
        s_edges = sem("edges_ready")
        s_xT = sem("xT_turned")
        s_xT_hi = sem("xT_hi")
        s_xT_lo = sem("xT_lo")
        s_drow = sem("dst_rows_ready")
        s_drow_hi = sem("dst_rows_hi")
        s_drow_lo = sem("dst_rows_lo")
        s_proj = sem("projected")
        s_xh_hi = sem("xh_hi")
        s_xh_lo = sem("xh_lo")
        s_z = sem("scores_ready")
        s_u = sem("masked_ready")
        s_neg_z = sem("neg_z_ready")
        s_src = sem("source_added")
        s_leaky = sem("leaky_done")
        s_p = sem("probs_ready")
        s_pT = sem("probs_turned")
        s_pT_hi = sem("probsT_hi")
        s_pT_lo = sem("probsT_lo")
        s_head = sem("head_summed")
        s_agg = sem("agg_ready")
        s_recip = sem("recip_ready")
        s_scaled = sem("heads_scaled")
        s_sd = sem("src_dst_ready")
        s_dT = sem("dst_turned")
        s_dT_hi = sem("dstT_hi")
        s_dT_lo = sem("dstT_lo")
        s_xa_hi = sem("xa_hi")
        s_xa_lo = sem("xa_lo")
        s_nT = sem("nT_turned")
        s_nT_hi = sem("nT_hi")
        s_nT_lo = sem("nT_lo")
        s_up = sem("up_ready")
        s_g = sem("gelu_full")
        s_g_hi = sem("gelu_hi")
        s_g_lo = sem("gelu_lo")
        s_down = sem("down_ready")
        s_hb_step = sem("residual_scaled")
        s_hb = sem("residual_ready")
        s_aff_step = sem("x_scaled")
        s_aff = sem("x_ready")
        s_sum = {k: sem(f"{k}_sum") for k in NORMS}
        s_stat = {k: sem(f"{k}_stats") for k in NORMS}
        s_var = {k: sem(f"{k}_meanvar") for k in NORMS}
        s_eps = {k: sem(f"{k}_vareps") for k in NORMS}
        s_rstd = {k: sem(f"{k}_rstd") for k in NORMS}
        s_norm = {k: sem(f"{k}_norm") for k in NORMS}
        s_out = [sem(f"out_stored{s}") for s in range(S)]

        block = ctx.enter_context(nc.Block())

        def f32(ap):
            return ap.bitcast(F32)

        def spread(ap, shape):
            return ap.broadcast_to(shape)

        def vector_waits(dve, semaphore, value):
            dve.wait_ge(semaphore, value)
            dve.memset(dve_mark[:, next(dve_marks)], 0.0)

        def pool_waits(pool, semaphore, value):
            pool.wait_ge(semaphore, value)
            pool.tensor_tensor(pool_mark[:, next(pool_marks)], half_neg[:, 0:1], half_neg[:, 0:1], ALU.mult)

        def all_partitions(ap, n):
            return ap.rearrange("(o n) -> o n", o=1).broadcast_to([P, n])

        def weight_blocks():
            for l in range(L):
                for part in range(KD):
                    yield True, l, part
                for part in range(2):
                    yield False, l, part

        HF = FT // 2
        blocks = list(weight_blocks())

        def stage_flat(b):
            return stage[b % 2][:, :, :].rearrange("p a n -> p (a n)")

        def weight_dst(b, t1, t2):
            up, l, part = blocks[b]
            if up:
                return t1[:, l, part, :]
            return t2[:, l, part * HF:(part + 1) * HF, :].rearrange("p f d -> p (f d)")

        @block.sync
        def _(sp):
            for b, (up, l, part) in enumerate(blocks):
                if b >= 2:
                    sp.wait_ge(s_hi_done, b - 1)
                    sp.wait_ge(s_lo_done, b - 1)
                if up:
                    src = W1[l, part * P:(part + 1) * P, :]
                    dst = stage_flat(b)
                else:
                    src = W2[l].rearrange("(f p) d -> p f d", p=P)[:, part * HF:(part + 1) * HF, :]
                    dst = stage_flat(b).rearrange("p (f d) -> p f d", f=HF)
                sp.dma_start(dst, src).then_inc(s_stage[b % 2], 16)
            sp.wait_ge(s_ready, 1)

            def load_x(it, s):
                g0 = it * (S * G) + s * G
                sp.dma_start(x0[:, s, :, :], x[bass.ds(g0, G), :, :].rearrange("g p d -> p g d"))\
                  .then_inc(s_x[s], 16)

            def load_adj(it, s):
                g0 = it * (S * G) + s * G
                sp.dma_start(adj_in[:, :, :], adj[bass.ds(g0, G), :, :].rearrange("g p d -> p g d"))\
                  .then_inc(s_adj, 16)

            def store(it, s):
                g0 = it * (S * G) + s * G
                sp.wait_ge(s_norm["end"], it * (S * G) + (s + 1) * G)
                sp.dma_start(out[bass.ds(g0, G), :, :].rearrange("g p d -> p g d"), xs[:, s, :, :])\
                  .then_inc(s_out[s], 16)

            load_x(0, 0)
            load_adj(0, 0)
            load_x(0, 1)
            sp.wait_ge(s_adj_used, 1)
            load_adj(0, 1)
            with sp.Fori(0, TURNS - 1) as it:
                for s in range(S):
                    sp.wait_ge(s_sum["end"], it * (S * G) + (s + 1) * G)
                    load_x(it + 1, s)
                    if s == 0:
                        sp.wait_ge(s_adj_used, it * S + S)
                        load_adj(it + 1, 0)
                    store(it, s)
                sp.wait_ge(s_adj_used, it * S + S + 1)
                load_adj(it + 1, 1)
            for s in range(S):
                store(TURNS - 1, s)
            for s in range(S):
                sp.wait_ge(s_out[s], 16 + 16 * TURNS)

        @block.gpsimd
        def _(pool):
            pool.dma_start(rows_in[0:NB, :], b1.rearrange("l (f p) -> (l f) p", p=P)).then_inc(s_rows, 16)
            pool.dma_start(rows_in[NB:NB + NK, :], g1.rearrange("l (k p) -> (l k) p", p=P)).then_inc(s_rows, 16)
            pool.dma_start(rows_in[NB + NK:NB + 2 * NK, :], beta1.rearrange("l (k p) -> (l k) p", p=P))\
                .then_inc(s_rows, 16)
            pool.memset(ident[:, :], 0.0).then_inc(s_made, 1)
            pool.wait_ge(s_made, 1)
            pool.affine_select(out=ident[:, :], in_=ident[:, :], compare_op=ALU.not_equal, fill=1.0,
                               base=0, pattern=[[-1, P]], channel_multiplier=1).then_inc(s_made, 1)
            pool.memset(half_neg[:, :], -0.5).then_inc(s_made, 1)
            pool.memset(f32(G_hi[:, :]), 0.0).then_inc(s_made, 1)
            pool.memset(f32(sel[:, :, :]), 0.0).then_inc(s_made, 1)
            pool.memset(f32(dst_row[:, :]), 0.0).then_inc(s_made, 1)
            pool.memset(f32(xa_hi[:, :, D:D + 1]), 1.0).then_inc(s_made, 1)
            pool.memset(f32(xa_hi[:, :, D + 1:D + 2]), 0.0).then_inc(s_made, 1)
            pool.memset(f32(xa_lo[:, :, D:D + 2]), 0.0).then_inc(s_made, 1)
            pool.wait_ge(s_ready, 1)

            def masks(it, s):
                pool_waits(pool, s_adj, it * (16 * S) + 16 * (s + 1))
                pool.tensor_scalar(edge0[:, s, :, :], adj_in[:, :, :], 0.0, MASKED, ALU.is_le, ALU.mult)
                pool.tensor_scalar(edge1[:, s, :, :], adj_in[:, :, :], 1.0, None, ALU.mult)\
                    .then_inc(s_adj_used, 1)
                pool.wait_ge(s_adj_used, it * S + s + 1)
                pool.tensor_tensor(edge1[:, s, :, :], edge1[:, s, :, :],
                                   spread(ident[:, :].rearrange("p (o n) -> p o n", o=1), [P, G, N]),
                                   ALU.add).then_inc(s_self, 1)
                pool_waits(pool, s_self, it * S + s + 1)
                pool.tensor_scalar(edge1[:, s, :, :], edge1[:, s, :, :], 0.0, MASKED, ALU.is_le, ALU.mult)\
                    .then_inc(s_edges, 1)

            def add_source(it, q, src):
                pool.wait_ge(s_u, it * Q + q + 1)
                if q >= 2:
                    pool.wait_ge(s_pT, it * Q + q - 1)
                b = q % 2
                pool.tensor_tensor(w[:, b, :].rearrange("p (g n) -> p g n", g=G),
                                   u[:, b, :].rearrange("p (g n) -> p g n", g=G),
                                   spread(src.rearrange("p (g o) -> p g o", o=1), [P, G, N]),
                                   ALU.add).then_inc(s_src, 1)

            def inverse_root(it, kind, per, n):
                pool.wait_ge(s_eps[kind], it * per + n + 1)
                pool.tensor_tensor(rstd[kind][:, :], vareps[kind][:, :], half_neg[:, :], ALU.pow)\
                    .then_inc(s_rstd[kind], 1)

            def residual(it, n):
                l, s = n // S, n % S
                pool.wait_ge(s_nT, it * (SLOTS * KD) + (n + 1) * KD)
                for g in range(G):
                    pool.tensor_tensor(xs[:, s, g, :], xs[:, s, g, :], gamma1[:, l, :], ALU.mult).then_inc(s_hb_step, 1)
                for g in range(G):
                    pool.wait_ge(s_hb_step, it * (SLOTS * G) + n * G + g + 1)
                    pool.tensor_tensor(xs[:, s, g, :], xs[:, s, g, :], shift1[:, l, :], ALU.add).then_inc(s_hb, 1)

            def affine(it, n):
                l, s = n // S, n % S
                for g in range(G):
                    pool.wait_ge(s_norm["n2"], it * (SLOTS * G) + n * G + g + 1)
                    pool.tensor_tensor(xs[:, s, g, :], xs[:, s, g, :], gamma2[:, l, :], ALU.mult).then_inc(s_aff_step, 1)
                    pool.wait_ge(s_aff_step, it * (SLOTS * G) + n * G + g + 1)
                    pool.tensor_tensor(xs[:, s, g, :], xs[:, s, g, :], shift2[:, l, :], ALU.add).then_inc(s_aff, 1)

            with pool.Fori(0, TURNS) as it:
                for s in range(S):
                    masks(it, s)
                    for h in range(H):
                        add_source(it, s * H + h, src0[:, :, h])
                    inverse_root(it, "l0", S, s)
                add_source(it, S * H, src1[:, :])
                inverse_root(it, "n1", SLOTS, 0)
                for n in range(SLOTS):
                    if n:
                        inverse_root(it, "n2", SLOTS, n - 1)
                        affine(it, n - 1)
                        if n - 1 >= SLOTS - S:
                            inverse_root(it, "end", S, n - 1 - (SLOTS - S))
                    residual(it, n)
                    if n + 1 < SLOTS:
                        add_source(it, S * H + n + 1, src1[:, :])
                        inverse_root(it, "n1", SLOTS, n + 1)
                inverse_root(it, "n2", SLOTS, SLOTS - 1)
                affine(it, SLOTS - 1)
                inverse_root(it, "end", S, S - 1)

        @block.scalar
        def _(act):
            act.dma_start(wp_in, w_proj.rearrange("(k p) d -> p k d", p=P)).then_inc(s_wp, 16)
            act.dma_start(watt_b, all_partitions(w_att.rearrange("h k -> (h k)"), H * K2)
                          .rearrange("p (h k) -> p h k", h=H)).then_inc(s_wp, 16)
            for dst, src, n in ((attw, attn_w, L * 2 * D), (gamma1, g1, L * D), (shift1, beta1, L * D),
                                (gamma2, g2, L * D), (shift2, beta2, L * D)):
                act.dma_start(dst[:, :, :].rearrange("p l d -> p (l d)"),
                              all_partitions(src.rearrange("l d -> (l d)"), n)).then_inc(s_consts, 16)
            act.dma_start(batt[:, :], all_partitions(b_att, H)).then_inc(s_consts, 16)
            act.dma_start(attb[:, :], all_partitions(attn_b, L)).then_inc(s_consts, 16)
            act.wait_ge(s_prep, 4 * KD)
            act.dma_start(b2_b.rearrange("p l d -> p (l d)"), all_partitions(b2.rearrange("l d -> (l d)"), L * D))\
               .then_inc(s_consts, 16)
            for b, (up, l, part) in enumerate(blocks):
                act.wait_ge(s_stage[b % 2], 16 * (b // 2 + 1))
                if up:
                    act.wait_ge(s_cols, 1)
                    c = NB + l * KD + part
                    act.activation(weight_dst(b, w1_hi, w2_hi), stage_flat(b), ACT.Identity,
                                   scale=cols[:, c:c + 1]).then_inc(s_hi_done, 1)
                else:
                    act.activation(weight_dst(b, w1_hi, w2_hi), stage_flat(b), ACT.Copy)\
                       .then_inc(s_hi_done, 1)

            def xT_hi(it, s):
                for k in range(KD):
                    act.wait_ge(s_xT, it * (S * KD) + s * KD + k + 1)
                    act.activation(nT_hi[:, k, :], [Z, T][k][:, :], ACT.Copy).then_inc(s_xT_hi, 1)

            def xh_parts(it, s):
                act.wait_ge(s_drow, it * S + s + 1)
                act.activation(dst_rows[0:H, :], U0[0:H, :], ACT.Copy).then_inc(s_drow_hi, 1)
                for g in range(G):
                    act.wait_ge(s_proj, it * (S * G) + s * G + g + 1)
                    act.activation(xh_hi[:, g, :, 0:KH],
                                   out0_bank[g][:, 0:D].rearrange("p (h c) -> p h c", h=H), ACT.Copy)\
                       .then_inc(s_xh_hi, 1)

            def exponential(it, q):
                act.wait_ge(s_leaky, it * Q + q + 1)
                b = q % 2
                for g in range(G):
                    c = slice(g * N, (g + 1) * N)
                    ins = act.activation(w[:, b, c], w[:, b, c], ACT.Exp, bias=neg_top[:, b, g:g + 1])
                ins.then_inc(s_p, 1)

            def probsT_hi(it, q):
                act.wait_ge(s_pT, it * Q + q + 1)
                heads = q < S * H
                act.activation(pT0_hi[q % 2] if heads else nT_hi[:, 0, :],
                               pT_bank[q % 2 if heads else 0][:, :], ACT.Copy).then_inc(s_pT_hi, 1)

            def dstT_hi(it, n):
                act.wait_ge(s_dT, it * SLOTS + n + 1)
                act.activation(dst_row[0:G, :], T[0:G, 0:P], ACT.Copy).then_inc(s_dT_hi, 1)

            def nT_hi_parts(it, n):
                for k in range(KD):
                    act.wait_ge(s_nT, it * (SLOTS * KD) + n * KD + k + 1)
                    act.activation(nT_hi[:, k, :], [Z, T][k][:, :], ACT.Copy).then_inc(s_nT_hi, 1)

            def xa_hi_parts(it, n):
                l, s = n // S, n % S
                src = x0 if l == 0 else xs
                if l == 0:
                    act.wait_ge(s_norm["l0"], it * (S * G) + (s + 1) * G)
                else:
                    act.wait_ge(s_aff, it * (SLOTS * G) + (n - S + 1) * G)
                if n:
                    act.wait_ge(s_agg, it * (SLOTS * G) + n * G)
                act.activation(xa_hi[:, :, 0:D], src[:, s, :, :], ACT.Copy).then_inc(s_xa_hi, 1)

            def attention(it, n):
                q = S * H + n
                dstT_hi(it, n)
                exponential(it, q)
                probsT_hi(it, q)
                nT_hi_parts(it, n)

            with act.Fori(0, TURNS) as it:
                for s in range(S):
                    xT_hi(it, s)
                    xh_parts(it, s)
                    for h in range(H + 1):
                        q = s * H + h
                        if h < H:
                            exponential(it, q)
                        if h:
                            probsT_hi(it, q - 1)
                xa_hi_parts(it, 0)
                attention(it, 0)
                for n in range(SLOTS):
                    l = n // S
                    for f in range(FT):
                        e = n * FT + f
                        act.wait_ge(s_up, it * (SLOTS * FT) + e + 1)
                        if e >= 2:
                            act.wait_ge(s_g_lo, it * (SLOTS * FT) + e - 1)
                        b = bias1[:, l * FT + f:l * FT + f + 1]
                        act.activation(g_full[:, f % 2, :], up_bank[f % 2][:, :], ACT.Gelu, bias=b)\
                           .then_inc(s_g, 1)
                        act.activation(Gh[:, f, :], up_bank[f % 2][:, :], ACT.Gelu, bias=b).then_inc(s_g_hi, 1)
                    if n + 1 < SLOTS:
                        xa_hi_parts(it, n + 1)
                        attention(it, n + 1)

        @block.tensor
        def _(pe):
            def split_matmul(dst, a_hi, a_lo, b_hi, b_lo, first, last):
                pe.matmul(dst, a_hi, b_hi, start=first, stop=False)
                pe.matmul(dst, a_hi, b_lo, start=False, stop=False)
                return pe.matmul(dst, a_lo, b_hi, start=False, stop=last)

            pe.wait_ge(s_made, 2)
            pe.wait_ge(s_rows, 48)
            nr = NB + 2 * NK
            pe.transpose(T[:, 0:nr], rows_in, ident[0:nr, 0:nr]).then_inc(s_cols_ps, 1)
            pe.wait_ge(s_cols, 1)
            done = 0
            for b, (up, l, part) in enumerate(blocks):
                if not up:
                    continue
                pe.wait_ge(s_stage[b % 2], 16 * (b // 2 + 1))
                c = NB + NK + l * KD + part
                for f in range(FT):
                    mm = pe.matmul([Z, U0][part][:, l * FT + f:l * FT + f + 1],
                                   stage_flat(b)[:, f * P:(f + 1) * P], cols[:, c:c + 1], start=True, stop=True)
                mm.then_inc(s_bmm, 1)
            pe.wait_ge(s_ready, 1)

            def transposes_to(banks, src, done_sem):
                for k in range(KD):
                    for g in range(G):
                        t = pe.transpose(banks[k][:, g * P:(g + 1) * P], src[:, g, k * P:(k + 1) * P], ident[:, :])
                    t.then_inc(done_sem, 1)

            def project(it, s):
                pe.wait_ge(s_x[s], it * 16 + 16)
                transposes_to([Z, T], x0[:, s, :, :], s_xT)
                pe.wait_ge(s_xT_lo, it * (S * KD) + (s + 1) * KD)
                for k in range(KD):
                    mm = split_matmul(U0[0:H, :], wp_hi[:, k, D + H:PW], wp_lo[:, k, D + H:PW],
                                      nT_hi[:, k, :], nT_lo[:, k, :], k == 0, k == KD - 1)
                mm.then_inc(s_drow, 1)
                if s == 0:
                    pe.wait_ge(s_sum["n2"], it * (SLOTS * G) + 1)
                for g in range(G):
                    if s:
                        pe.wait_ge(s_scaled, it * (S * G) + (s - 1) * G + g + 1)
                    c = slice(g * P, (g + 1) * P)
                    for k in range(KD):
                        mm = split_matmul(out0_bank[g][:, 0:D + H], nT_hi[:, k, c], nT_lo[:, k, c],
                                          wp_hi[:, k, 0:D + H], wp_lo[:, k, 0:D + H], k == 0, k == KD - 1)
                    mm.then_inc(s_proj, 1)

            def head_scores(it, s, h):
                if h == 0:
                    pe.wait_ge(s_drow_lo, it * S + s + 1)
                pe.matmul(z_bank[h % 2][:, :], sel[:, h, :], dst_rows, start=True, stop=True).then_inc(s_z, 1)

            def turn_probs(it, q, dst):
                pe.wait_ge(s_p, it * Q + q + 1)
                for g in range(G):
                    t = pe.transpose(dst[:, g * P:(g + 1) * P], w[:, q % 2, g * P:(g + 1) * P], ident[:, :])
                t.then_inc(s_pT, 1)

            def head_sum(it, s, h):
                q = s * H + h
                if h == 0:
                    pe.wait_ge(s_xh_lo, it * (S * G) + (s + 1) * G)
                pe.wait_ge(s_pT_lo, it * Q + q + 1)
                for g in range(G):
                    c = slice(g * P, (g + 1) * P)
                    mm = split_matmul(out0_bank[g][:, h * HW:(h + 1) * HW], pT0_hi[h % 2][:, c], pT0_lo[h % 2][:, c],
                                      xh_hi[:, g, h, :], xh_lo[:, g, h, :], True, True)
                mm.then_inc(s_head, 1)

            def dst_scores(it, n):
                pe.wait_ge(s_sd, it * (SLOTS * G) + (n + 1) * G)
                pe.transpose(T[0:G, 0:P], dst1[:, :], ident[:, :]).then_inc(s_dT, 1)
                pe.wait_ge(s_dT_lo, it * SLOTS + n + 1)
                for g in range(G):
                    mm = pe.matmul(Z[:, g * P:(g + 1) * P], sel[0:32 + G, g, :], dst_row[0:32 + G, :],
                                   start=True, stop=True)
                mm.then_inc(s_z, 1)

            def aggregate(it, n):
                q = S * H + n
                pe.wait_ge(s_xa_lo, it * SLOTS + n + 1)
                pe.wait_ge(s_pT_lo, it * Q + q + 1)
                for g in range(G):
                    if g >= 2:
                        pe.wait_ge(s_sum["n1"], it * (SLOTS * G) + n * G + g - 1)
                    c = slice(g * P, (g + 1) * P)
                    split_matmul(agg_bank[g % 2][:, 0:XW], nT_hi[:, 0, c], nT_lo[:, 0, c],
                                 xa_hi[:, g, :], xa_lo[:, g, :], True, True).then_inc(s_agg, 1)

            def turn_norm(it, n):
                pe.wait_ge(s_norm["n1"], it * (SLOTS * G) + (n + 1) * G)
                transposes_to([Z, T], xs[:, n % S, :, :], s_nT)

            def up(it, n):
                l = n // S
                for f in range(FT):
                    e = n * FT + f
                    c = slice(f * P, (f + 1) * P)
                    if f == 0:
                        pe.wait_ge(s_nT_lo, it * (SLOTS * KD) + n * KD + 1)
                    if e >= 2:
                        pe.wait_ge(s_g_hi, it * (SLOTS * FT) + e - 1)
                    for k in range(KD):
                        if f == 0 and k == KD - 1:
                            pe.wait_ge(s_nT_lo, it * (SLOTS * KD) + (n + 1) * KD)
                        mm = split_matmul(up_bank[f % 2][:, :], w1_hi[:, l, k, c], w1_lo[:, l, k, c],
                                          nT_hi[:, k, :], nT_lo[:, k, :], k == 0, k == KD - 1)
                    mm.then_inc(s_up, 1)

            def down(it, n, g):
                l = n // S
                c = slice(g * P, (g + 1) * P)
                e = n * G + g
                if n == 0 and g < 2:
                    pe.wait_ge(s_scaled, it * (S * G) + S * G)
                else:
                    pe.wait_ge(s_sum["n2"], it * (SLOTS * G) + 1 + e - 1)
                for f in range(FT):
                    if g == 0:
                        pe.wait_ge(s_g_lo, it * (SLOTS * FT) + n * FT + f + 1)
                    mm = split_matmul(down_bank[g % 2][:, 0:D], Gh[:, f, c], Gl[:, f, c],
                                      w2_hi[:, l, f, :], w2_lo[:, l, f, :], f == 0, f == FT - 1)
                mm.then_inc(s_down, 1)

            with pe.Fori(0, TURNS) as it:
                for s in range(S):
                    project(it, s)
                    head_scores(it, s, 0)
                    head_scores(it, s, 1)
                    for h in range(H + 1):
                        if h < H:
                            turn_probs(it, s * H + h, pT_bank[h % 2])
                        if h + 2 < H:
                            head_scores(it, s, h + 2)
                        if h:
                            head_sum(it, s, h - 1)
                dst_scores(it, 0)
                turn_probs(it, S * H, T)
                aggregate(it, 0)
                turn_norm(it, 0)
                for n in range(SLOTS):
                    up(it, n)
                    more = n + 1 < SLOTS
                    if more:
                        dst_scores(it, n + 1)
                    down(it, n, 0)
                    down(it, n, 1)
                    if more:
                        turn_probs(it, S * H + n + 1, T)
                    down(it, n, 2)
                    if more:
                        aggregate(it, n + 1)
                    down(it, n, 3)
                    if more:
                        turn_norm(it, n + 1)

        @block.vector
        def _(dve):
            steps = [0]

            def prep(ins):
                steps[0] += 1
                ins.then_inc(s_prep, 1)
                dve.wait_ge(s_prep, steps[0])

            dve.wait_ge(s_wp, 32)
            for k in range(KD):
                for side in range(2):
                    prep(dve.tensor_tensor(prod.rearrange("p (h c) -> p h c", h=H),
                                           wp_in[:, k, :].rearrange("p (h c) -> p h c", h=H),
                                           watt_b[:, :, side * KH:(side + 1) * KH], ALU.mult))
                    prep(dve.tensor_reduce(wsum[:, k, side * H:(side + 1) * H],
                                           prod.rearrange("p (h c) -> p h c", h=H), AX_X, ALU.add))
            for part, src in ((slice(0, D), wp_in), (slice(D, PW), wsum)):
                prep(dve.tensor_copy(wp_hi[:, :, part], src))
                prep(dve.tensor_tensor(wp_lo[:, :, part], src, f32(wp_hi[:, :, part]), ALU.subtract))
            dve.wait_ge(s_cols_ps, 1)
            dve.tensor_copy(cols[:, :], T[:, 0:NB + 2 * NK]).then_inc(s_cols, 1)
            dve.wait_ge(s_made, 9)
            for first in (0, 32):
                some = slice(first, first + H)
                prep(dve.tensor_copy(sel[some, :, :],
                                     spread(ident[some, some].rearrange("p (h o) -> p h o", o=1), [H, H, P])))
            dve.wait_ge(s_cols, 1)
            n_up = 0
            for b, (is_up, l, part) in enumerate(blocks):
                dve.wait_ge(s_hi_done, b + 1)
                hi, lo = weight_dst(b, w1_hi, w2_hi), weight_dst(b, w1_lo, w2_lo)
                if is_up:
                    n_up += 1
                    dve.wait_ge(s_bmm, n_up)
                    c = NB + l * KD + part
                    dve.scalar_tensor_tensor(lo, stage_flat(b), cols[:, c:c + 1], f32(hi),
                                             ALU.mult, ALU.subtract).then_inc(s_lo_done, 1)
                else:
                    dve.tensor_tensor(lo, stage_flat(b), f32(hi), ALU.subtract).then_inc(s_lo_done, 1)
            prep(dve.tensor_tensor(bias1_part[:, :], Z[:, 0:NB], cols[:, 0:NB], ALU.add))
            prep(dve.tensor_tensor(bias1[:, :], U0[:, 0:NB], bias1_part[:, :], ALU.add))
            dve.wait_ge(s_consts, 16 * 8)
            prep(dve.tensor_tensor(shift1[:, :, :], shift1[:, :, :], b2_b, ALU.add))
            dve.tensor_copy(recip1[:, 0:1], attb[:, 0:1]).then_inc(s_sum["n2"], 1)
            for s in range(S):
                dve.tensor_copy(recip1[:, 1 + s:2 + s], attb[:, 0:1]).then_inc(s_out[s], 16)
            dve.tensor_copy(recip1[:, 3:4], attb[:, 0:1]).then_inc(s_ready, 1)

            def low_part(dst, src, hi):
                return dve.tensor_tensor(dst, src, f32(hi), ALU.subtract)

            def xT_lo(it, s):
                for k in range(KD):
                    dve.wait_ge(s_xT_hi, it * (S * KD) + s * KD + k + 1)
                    low_part(nT_lo[:, k, :], [Z, T][k][:, :], nT_hi[:, k, :]).then_inc(s_xT_lo, 1)

            def xh_parts(it, s):
                dve.wait_ge(s_drow_hi, it * S + s + 1)
                if s == 0:
                    dve.memset(f32(xh_hi[:, :, :, KH:KH + 1]), 1.0)
                    dve.memset(f32(xh_hi[:, :, :, KH + 1:HW]), 0.0)
                    dve.memset(f32(xh_lo[:, :, :, KH:HW]), 0.0)
                low_part(dst_rows[32:32 + H, :], U0[0:H, :], dst_rows[0:H, :]).then_inc(s_drow_lo, 1)
                for g in range(G):
                    dve.wait_ge(s_xh_hi, it * (S * G) + s * G + g + 1)
                    low_part(xh_lo[:, g, :, 0:KH], out0_bank[g][:, 0:D].rearrange("p (h c) -> p h c", h=H),
                             xh_hi[:, g, :, 0:KH])
                    dve.tensor_tensor(src0[:, g, :], out0_bank[g][:, D:D + H], batt[:, :], ALU.add)\
                       .then_inc(s_xh_lo, 1)

            def masked_scores(it, q, bank_, edge, src):
                b = q % 2
                if q >= 2:
                    dve.wait_ge(s_src, it * Q + q - 1)
                vector_waits(dve, s_z, it * Q + q + 1)
                for g in range(G):
                    ins = dve.tensor_tensor_reduce(
                        out=u[:, b, g * N:(g + 1) * N], in0=bank_[:, g * N:(g + 1) * N], in1=edge[:, g, :],
                        scale=1.0, scalar=-3.0e38, op0=ALU.add, op1=ALU.max, accum_out=row_max[:, g:g + 1])
                ins.then_inc(s_u, 1)
                dve.wait_ge(s_u, it * Q + q + 1)
                dve.scalar_tensor_tensor(neg_z[:, :], row_max[:, :], -1.0, src, ALU.mult, ALU.subtract)\
                   .then_inc(s_neg_z, 1)
                dve.wait_ge(s_neg_z, it * Q + q + 1)
                dve.scalar_tensor_tensor(neg_top[:, b, :], neg_z[:, :], SLOPE, neg_z[:, :], ALU.mult, ALU.min)

            def leaky(it, q):
                dve.wait_ge(s_src, it * Q + q + 1)
                dve.scalar_tensor_tensor(w[:, q % 2, :], w[:, q % 2, :], SLOPE, w[:, q % 2, :],
                                         ALU.mult, ALU.max).then_inc(s_leaky, 1)

            def probsT_lo(it, q):
                heads = q < S * H
                dve.wait_ge(s_pT_hi, it * Q + q + 1)
                low_part(pT0_lo[q % 2] if heads else nT_lo[:, 0, :], pT_bank[q % 2 if heads else 0][:, :],
                         pT0_hi[q % 2] if heads else nT_hi[:, 0, :]).then_inc(s_pT_lo, 1)

            def row_stats(it, kind, per, n, g, rows):
                e = it * (per * G) + n * G + g + (1 if kind == "n2" else 0)
                dve.wait_ge(s_sum[kind], e + 1)
                dve.bn_stats(stats[kind][:, g, :], rows).then_inc(s_stat[kind], 1)

            def mean_var(it, kind, per, n):
                for g in range(G):
                    if g == 0:
                        vector_waits(dve, s_stat[kind], it * (per * G) + (n + 1) * G)
                    ins = dve.bn_aggr(meanvar[kind][:, g, :], stats[kind][:, g, :])
                ins.then_inc(s_var[kind], 1)
                dve.wait_ge(s_var[kind], it * per + n + 1)
                dve.tensor_scalar(vareps[kind][:, :], meanvar[kind][:, :, 1], EPS, None, ALU.add)\
                   .then_inc(s_eps[kind], 1)

            def normalize(it, kind, per, n, g, dst, rows):
                if g == 0:
                    dve.wait_ge(s_rstd[kind], it * per + n + 1)
                dve.tensor_scalar(dst, rows, meanvar[kind][:, g, 0:1], rstd[kind][:, g:g + 1],
                                  ALU.subtract, ALU.mult).then_inc(s_norm[kind], 1)

            RN = (S + SLOTS) * G

            def heads_norm(it, s):
                dve.wait_ge(s_head, it * (S * H) + (s + 1) * H)
                dve.wait_ge(s_out[s], it * 16 + 16)
                for g in range(G):
                    heads = out0_bank[g][:, 0:H * HW].rearrange("p (h c) -> p h c", h=H)
                    e = it * (S * G) + s * G + g + 1
                    dve.reciprocal(recip0[:, g, :], heads[:, :, KH]).then_inc(s_recip, 1)
                    dve.wait_ge(s_recip, it * RN + s * G + g + 1)
                    rows = xs[:, s, g, :]
                    dve.tensor_tensor(rows.rearrange("p (h c) -> p h c", h=H), heads[:, :, 0:KH],
                                      spread(recip0[:, g, :].rearrange("p (h o) -> p h o", o=1), [P, H, KH]),
                                      ALU.mult).then_inc(s_scaled, 1)
                    dve.wait_ge(s_scaled, e)
                    dve.scalar_tensor_tensor(rows, rows, 0.0, x0[:, s, g, :], ALU.max, ALU.add)\
                       .then_inc(s_sum["l0"], 1)
                    row_stats(it, "l0", S, s, g, rows)
                mean_var(it, "l0", S, s)
                for g in range(G):
                    normalize(it, "l0", S, s, g, x0[:, s, g, :], xs[:, s, g, :])

            def src_dst(it, n, g):
                l, s = n // S, n % S
                rows = (x0 if l == 0 else xs)[:, s, g, :]
                if l == 0:
                    dve.wait_ge(s_norm["l0"], it * (S * G) + s * G + g + 1)
                else:
                    dve.wait_ge(s_aff, it * (SLOTS * G) + (n - S) * G + g + 1)
                if g:
                    dve.wait_ge(s_sd, it * (SLOTS * G) + n * G + g)
                junk, junk2 = (w[:, (n + 1) % 2, i * D:(i + 1) * D] for i in range(2))
                dve.tensor_tensor_reduce(out=junk, in0=rows, in1=attw[:, l, 0:D], scale=1.0,
                                         scalar=attb[:, l:l + 1], op0=ALU.mult, op1=ALU.add,
                                         accum_out=src1[:, g:g + 1])
                dve.tensor_tensor_reduce(out=junk2, in0=rows, in1=attw[:, l, D:2 * D], scale=1.0,
                                         scalar=0.0, op0=ALU.mult, op1=ALU.add,
                                         accum_out=dst1[:, g:g + 1]).then_inc(s_sd, 1)

            def xa_lo_parts(it, n):
                l, s = n // S, n % S
                dve.wait_ge(s_xa_hi, it * SLOTS + n + 1)
                low_part(xa_lo[:, :, 0:D], (x0 if l == 0 else xs)[:, s, :, :], xa_hi[:, :, 0:D]).then_inc(s_xa_lo, 1)

            def dstT_lo(it, n):
                dve.wait_ge(s_dT_hi, it * SLOTS + n + 1)
                low_part(dst_row[32:32 + G, :], T[0:G, 0:P], dst_row[0:G, :]).then_inc(s_dT_lo, 1)

            def attention_norm(it, n):
                l, s = n // S, n % S
                x_in = x0 if l == 0 else xs
                for g in range(G):
                    dve.wait_ge(s_agg, it * (SLOTS * G) + n * G + g + 1)
                    dve.reciprocal(recip1[:, g:g + 1], agg_bank[g % 2][:, D:D + 1]).then_inc(s_recip, 1)
                    dve.wait_ge(s_recip, it * RN + (S + n) * G + g + 1)
                    dve.scalar_tensor_tensor(xs[:, s, g, :], agg_bank[g % 2][:, 0:D], recip1[:, g:g + 1],
                                             x_in[:, s, g, :], ALU.mult, ALU.add).then_inc(s_sum["n1"], 1)
                    row_stats(it, "n1", SLOTS, n, g, xs[:, s, g, :])
                mean_var(it, "n1", SLOTS, n)
                for g in range(G):
                    normalize(it, "n1", SLOTS, n, g, xs[:, s, g, :], xs[:, s, g, :])

            def nT_lo_parts(it, n):
                for k in range(KD):
                    dve.wait_ge(s_nT_hi, it * (SLOTS * KD) + n * KD + k + 1)
                    low_part(nT_lo[:, k, :], [Z, T][k][:, :], nT_hi[:, k, :]).then_inc(s_nT_lo, 1)

            def feed_forward_sum(it, n, g):
                s = n % S
                dve.wait_ge(s_down, it * (SLOTS * G) + n * G + g + 1)
                dve.wait_ge(s_hb, it * (SLOTS * G) + n * G + g + 1)
                dve.tensor_tensor(xs[:, s, g, :], down_bank[g % 2][:, 0:D], xs[:, s, g, :], ALU.add)\
                   .then_inc(s_sum["n2"], 1)
                row_stats(it, "n2", SLOTS, n, g, xs[:, s, g, :])

            def feed_forward_norm(it, n):
                for g in range(G):
                    normalize(it, "n2", SLOTS, n, g, xs[:, n % S, g, :], xs[:, n % S, g, :])

            def end_sum(it, s, g):
                dve.wait_ge(s_aff, it * (SLOTS * G) + (SLOTS - S + s) * G + g + 1)
                dve.tensor_tensor(xs[:, s, g, :], xs[:, s, g, :], x0[:, s, g, :], ALU.add)\
                   .then_inc(s_sum["end"], 1)
                row_stats(it, "end", S, s, g, xs[:, s, g, :])

            def end_norm(it, s):
                for g in range(G):
                    normalize(it, "end", S, s, g, xs[:, s, g, :], xs[:, s, g, :])

            with dve.Fori(0, TURNS) as it:
                for s in range(S):
                    xT_lo(it, s)
                    xh_parts(it, s)
                    vector_waits(dve, s_edges, it * S + s + 1)
                    for h in range(H + 2):
                        if h < H:
                            masked_scores(it, s * H + h, z_bank[h % 2], edge0[:, s, :, :], src0[:, :, h])
                        if 1 <= h <= H:
                            leaky(it, s * H + h - 1)
                        if h >= 2:
                            probsT_lo(it, s * H + h - 2)
                    heads_norm(it, s)
                for g in range(G):
                    src_dst(it, 0, g)
                xa_lo_parts(it, 0)
                for n in range(-1, SLOTS):
                    m = n + 1
                    if n >= 0:
                        for f in range(FT):
                            if f == 0 and n:
                                feed_forward_norm(it, n - 1)
                            dve.wait_ge(s_g_hi, it * (SLOTS * FT) + n * FT + f + 1)
                            low_part(Gl[:, f, :], g_full[:, f % 2, :], Gh[:, f, :]).then_inc(s_g_lo, 1)
                            g = f - 2
                            if 0 <= g < G:
                                if n - 1 >= SLOTS - S:
                                    end_sum(it, n - 1 - (SLOTS - S), g)
                                    if g == G - 1:
                                        mean_var(it, "end", S, n - 1 - (SLOTS - S))
                                elif m < SLOTS and m >= 1:
                                    src_dst(it, m, g)
                        if n - 1 >= SLOTS - S:
                            end_norm(it, n - 1 - (SLOTS - S))
                        if m < SLOTS:
                            xa_lo_parts(it, m)
                    if m < SLOTS:
                        dstT_lo(it, m)
                        masked_scores(it, S * H + m, Z, edge1[:, m % S, :, :], src1[:, :])
                        leaky(it, S * H + m)
                    if n >= 0:
                        feed_forward_sum(it, n, 0)
                        feed_forward_sum(it, n, 1)
                    if m < SLOTS:
                        probsT_lo(it, S * H + m)
                    if n >= 0:
                        feed_forward_sum(it, n, 2)
                    if m < SLOTS:
                        attention_norm(it, m)
                        nT_lo_parts(it, m)
                    if n >= 0:
                        feed_forward_sum(it, n, 3)
                        mean_var(it, "n2", SLOTS, n)
                feed_forward_norm(it, SLOTS - 1)
                for g in range(G):
                    end_sum(it, S - 1, g)
                mean_var(it, "end", S, S - 1)
                end_norm(it, S - 1)


_INS = ['x', 'adj', 'L0_gnn_W_proj', 'L0_gnn_W_att', 'L0_gnn_b_att', 'L1_gnn_attn_w', 'L1_gnn_attn_b',
        'L1_gnn_W1', 'L1_gnn_b1', 'L1_gnn_W2', 'L1_gnn_b2', 'L1_gnn_g1', 'L1_gnn_beta1', 'L1_gnn_g2',
        'L1_gnn_beta2']
_OUTS = [((64, 128, 256), 'float32')]


def kernel(**inputs):
    import numpy as _np
    import concourse.bacc as _bacc
    from concourse import mybir as _mybir
    from concourse.bass_utils import run_bass_kernel_spmd as _run

    nc = _bacc.Bacc("TRN2", target_bir_lowering=False, num_devices=1)
    arrays, args = {}, []
    for name in _INS:
        a = _np.ascontiguousarray(inputs[name])
        arrays[f"in_{name}_dram"] = a
        args.append(nc.dram_tensor(f"in_{name}_dram", a.shape, _mybir.dt.from_np(a.dtype),
                                   kind="ExternalInput").ap())
    for i, (shape, dtype) in enumerate(_OUTS):
        dt = _mybir.dt.from_np(_np.dtype(dtype))
        args.append(nc.dram_tensor(f"out_{i}_dram", shape, dt, kind="ExternalOutput").ap())
    graph_network(nc, *args)
    r = _run(nc, [arrays], core_ids=[0])
    return r.results[0]["out_0_dram"]
```

```python
from contextlib import ExitStack

import concourse.bass as bass
from concourse import mybir

F32 = mybir.dt.float32
F32R = mybir.dt.float32r
BF16 = mybir.dt.bfloat16
I32 = mybir.dt.int32
ALU = mybir.AluOpType
ACT = mybir.ActivationFunctionType
AX_X = mybir.AxisListType.X

EPS = 1e-5
SLOPE = 0.2
MASKED = -(2.0 ** 100)


def graph_network(nc, x, adj, w_proj, w_att, b_att, attn_w, attn_b, W1, b1, W2, b2,
                  g1, beta1, g2, beta2, out):
    B, N, D = x.shape
    H, K2 = w_att.shape
    KH = K2 // 2
    L = attn_w.shape[0]
    F = W1.shape[2]
    P = N
    G = 4
    S = 2
    TURNS = B // (G * S)
    KD = D // P
    FT = F // P
    NG = G * N
    HW = KH + 2
    XW = D + 2
    assert P == 128 and NG == 512 and H * KH == D and KD == 2

    SLOTS = S * L
    Q = S * H + SLOTS

    def slot(l, s):
        return S * l + s

    with ExitStack() as ctx:
        def sb(name, shape, dt=F32):
            return ctx.enter_context(nc.sbuf_tensor(name, shape, dt))

        def sem(name):
            return ctx.enter_context(nc.semaphore(name))

        w1_hi, w1_lo = (sb(f"w1_{p}", [P, L, KD, F], F32R) for p in ("hi", "lo"))
        w2_hi, w2_lo = (sb(f"w2_{p}", [P, L, FT, D], F32R) for p in ("hi", "lo"))
        PW = D + 2 * H
        wp_hi, wp_lo = (sb(f"wp_{p}", [P, KD, PW], F32R) for p in ("hi", "lo"))
        attw = sb("attw", [P, L, 2 * D])
        gamma1 = sb("gamma1", [P, L, D])
        shift1 = sb("shift1", [P, L, D])
        gamma2 = sb("gamma2", [P, L, D])
        shift2 = sb("shift2", [P, L, D])
        NB, NK = L * FT, L * KD
        cols = sb("cols", [P, NB + 2 * NK])
        bias1 = sb("bias1", [P, NB])
        bias1_part = sb("bias1_part", [P, NB])
        batt = sb("batt", [P, H])
        attb = sb("attb", [P, L])
        ident = sb("ident", [P, P])
        sel = sb("sel", [32 + H, H, P], F32R)
        half_neg = sb("half_neg", [P, G])

        MARKS = 48
        dve_mark = sb("dve_mark", [P, MARKS])
        pool_mark = sb("pool_mark", [P, MARKS])
        dve_marks, pool_marks = (iter([slice(i, i + 1) for i in range(MARKS)]) for _ in range(2))

        x0 = sb("x0", [P, S, G, D])
        xs = sb("xs", [P, S, G, D])
        adj_in = sb("adj_in", [P, G, N], I32)
        edge0 = sb("edge0", [P, S, G, N], BF16)
        edge1 = sb("edge1", [P, S, G, N], BF16)
        xa_hi, xa_lo = (sb(f"xa_{p}", [P, G, XW], F32R) for p in ("hi", "lo"))
        nT_hi, nT_lo = (sb(f"nT_{p}", [P, KD, NG], F32R) for p in ("hi", "lo"))
        G_hi, G_lo = (sb(f"G_{p}", [P, FT * NG], F32R) for p in ("hi", "lo"))
        g_full = sb("g_full", [P, 2, NG])
        u = sb("u", [P, 2, NG])
        w = sb("w", [P, 2, NG])
        row_max = sb("row_max", [P, G])
        neg_z = sb("neg_z", [P, G])
        neg_top = sb("neg_top", [P, 4, G])
        src0 = sb("src0", [P, G, H])
        src1 = sb("src1", [P, G])
        dst1 = sb("dst1", [P, G])
        dst_row = sb("dst_row", [32 + H, P], F32R)
        recip0 = sb("recip0", [P, G, H])
        recip1 = sb("recip1", [P, G])
        NORMS = ("l0", "n1", "n2", "end")
        stats = {k: sb(f"stats_{k}", [P, G, 6]) for k in NORMS}
        meanvar = {k: sb(f"meanvar_{k}", [P, G, 2]) for k in NORMS}
        vareps = {k: sb(f"vareps_{k}", [P, G]) for k in NORMS}
        rstd = {k: sb(f"rstd_{k}", [P, G]) for k in NORMS}

        Gh = G_hi[:, :].rearrange("p (f n) -> p f n", f=FT)
        Gl = G_lo[:, :].rearrange("p (f n) -> p f n", f=FT)
        pT0_hi = [Gh[:, i, :] for i in range(2)]
        pT0_lo = [Gl[:, i, :] for i in range(2)]
        xh_hi = G_hi[:, 2 * NG:2 * NG + G * H * HW].rearrange("p (g h c) -> p g h c", g=G, h=H)
        xh_lo = G_lo[:, 2 * NG:2 * NG + G * H * HW].rearrange("p (g h c) -> p g h c", g=G, h=H)
        dst_rows = G_hi[0:32 + H, 5 * NG:6 * NG]
        stage = [u, w]
        watt_b = xs[:, 0, 0:2, :].rearrange("p a b -> p (a b)")[:, 0:H * K2].rearrange("p (h k) -> p h k", h=H)
        prod = xs[:, 1, 0, :]
        wp_in = x0[:, 0, 0:KD, :]
        wsum = x0[:, 1, 0:KD, 0:2 * H]
        rows_in = xs[0:NB + 2 * NK, 1, 1, 0:P]
        b2_b = xs[:, 0, 0:L, :]

        bank = [ctx.enter_context(nc.psum_tensor(f"bank{i}", [P, 512], F32)) for i in range(8)]
        U0, U1, V0, V1, Z, T, R0, R1 = bank
        up_bank = [U0, U1]
        down_bank = [V0, V1]
        agg_bank = [R0, R1]
        out0_bank = [R0, R1, V0, V1]
        z_bank = [Z, U0]
        pT_bank = [T, U1]

        DST_AT, SCORES_AT = 3, 5
        HI_BY_ACT = 6

        s_rows = sem("rows_loaded")
        s_consts = sem("consts_loaded")
        s_wp = sem("proj_loaded")
        s_stage = [sem(f"stage_loaded{i}") for i in range(2)]
        s_made = sem("pool_consts_made")
        s_prep = sem("prep_step")
        s_cols_ps = sem("columns_turned")
        s_cols = sem("columns_ready")
        s_bmm = sem("beta_product_done")
        s_hi_done = sem("weight_hi_done")
        s_lo_done = sem("weight_lo_done")
        s_ready = sem("weights_ready")
        s_x = [sem(f"x_loaded{s}") for s in range(S)]
        s_adj = sem("adj_loaded")
        s_adj_used = sem("adj_used")
        s_self = sem("self_edges_added")
        s_edges = sem("edges_ready")
        s_xT = sem("xT_turned")
        s_xT_hi = sem("xT_hi")
        s_xT_lo = sem("xT_lo")
        s_drow = sem("dst_rows_ready")
        s_drow_hi = sem("dst_rows_hi")
        s_drow_lo = sem("dst_rows_lo")
        s_proj = sem("projected")
        s_xh_hi = sem("xh_hi")
        s_xh_lo = sem("xh_lo")
        s_z = sem("scores_ready")
        s_u = sem("masked_ready")
        s_neg_z = sem("neg_z_ready")
        s_src = sem("source_added")
        s_leaky = sem("leaky_done")
        s_p = sem("probs_ready")
        s_pT = sem("probs_turned")
        s_pT_hi = sem("probsT_hi")
        s_pT_lo = sem("probsT_lo")
        s_head = sem("head_summed")
        s_agg = sem("agg_ready")
        s_recip = sem("recip_ready")
        s_scaled = sem("heads_scaled")
        s_sd = sem("src_dst_ready")
        s_dT = sem("dst_turned")
        s_dT_hi = sem("dstT_hi")
        s_dT_lo = sem("dstT_lo")
        s_xa_hi = sem("xa_hi")
        s_xa_lo = sem("xa_lo")
        s_nT = sem("nT_turned")
        s_nT_hi = sem("nT_hi")
        s_nT_lo = sem("nT_lo")
        s_up = sem("up_ready")
        s_g = sem("gelu_full")
        s_g_hi = sem("gelu_hi")
        s_g_lo = sem("gelu_lo")
        s_down = sem("down_ready")
        s_hb_step = sem("residual_scaled")
        s_hb = sem("residual_ready")
        s_aff_step = sem("x_scaled")
        s_aff = sem("x_ready")
        s_sum = {k: sem(f"{k}_sum") for k in NORMS}
        s_stat = {k: sem(f"{k}_stats") for k in NORMS}
        s_var = {k: sem(f"{k}_meanvar") for k in NORMS}
        s_eps = {k: sem(f"{k}_vareps") for k in NORMS}
        s_rstd = {k: sem(f"{k}_rstd") for k in NORMS}
        s_norm = {k: sem(f"{k}_norm") for k in NORMS}
        s_out = [sem(f"out_stored{s}") for s in range(S)]

        block = ctx.enter_context(nc.Block())

        def f32(ap):
            return ap.bitcast(F32)

        def spread(ap, shape):
            return ap.broadcast_to(shape)

        def vector_waits(dve, semaphore, value):
            dve.wait_ge(semaphore, value)
            dve.memset(dve_mark[:, next(dve_marks)], 0.0)

        def pool_waits(pool, semaphore, value):
            pool.wait_ge(semaphore, value)
            pool.tensor_tensor(pool_mark[:, next(pool_marks)], half_neg[:, 0:1], half_neg[:, 0:1], ALU.mult)

        def all_partitions(ap, n):
            return ap.rearrange("(o n) -> o n", o=1).broadcast_to([P, n])

        def weight_blocks():
            for l in range(L):
                for part in range(KD):
                    yield True, l, part
                for part in range(2):
                    yield False, l, part

        HF = FT // 2
        blocks = list(weight_blocks())

        def stage_flat(b):
            return stage[b % 2][:, :, :].rearrange("p a n -> p (a n)")

        def weight_dst(b, t1, t2):
            up, l, part = blocks[b]
            if up:
                return t1[:, l, part, :]
            return t2[:, l, part * HF:(part + 1) * HF, :].rearrange("p f d -> p (f d)")

        @block.sync
        def _(sp):
            for b, (up, l, part) in enumerate(blocks):
                if b >= 2:
                    sp.wait_ge(s_hi_done, b - 1)
                    sp.wait_ge(s_lo_done, b - 1)
                if up:
                    src = W1[l, part * P:(part + 1) * P, :]
                    dst = stage_flat(b)
                else:
                    src = W2[l].rearrange("(f p) d -> p f d", p=P)[:, part * HF:(part + 1) * HF, :]
                    dst = stage_flat(b).rearrange("p (f d) -> p f d", f=HF)
                sp.dma_start(dst, src).then_inc(s_stage[b % 2], 16)
            sp.wait_ge(s_ready, 1)

            def load_x(it, s):
                g0 = it * (S * G) + s * G
                sp.dma_start(x0[:, s, :, :], x[bass.ds(g0, G), :, :].rearrange("g p d -> p g d"))\
                  .then_inc(s_x[s], 16)

            def load_adj(it, s):
                g0 = it * (S * G) + s * G
                sp.dma_start(adj_in[:, :, :], adj[bass.ds(g0, G), :, :].rearrange("g p d -> p g d"))\
                  .then_inc(s_adj, 16)

            def store(it, s):
                g0 = it * (S * G) + s * G
                sp.wait_ge(s_norm["end"], it * (S * G) + (s + 1) * G)
                sp.dma_start(out[bass.ds(g0, G), :, :].rearrange("g p d -> p g d"), xs[:, s, :, :])\
                  .then_inc(s_out[s], 16)

            load_x(0, 0)
            load_adj(0, 0)
            load_x(0, 1)
            sp.wait_ge(s_adj_used, 1)
            load_adj(0, 1)
            with sp.Fori(0, TURNS - 1) as it:
                for s in range(S):
                    sp.wait_ge(s_sum["end"], it * (S * G) + (s + 1) * G)
                    load_x(it + 1, s)
                    if s == 0:
                        sp.wait_ge(s_adj_used, it * S + S)
                        load_adj(it + 1, 0)
                    store(it, s)
                sp.wait_ge(s_adj_used, it * S + S + 1)
                load_adj(it + 1, 1)
            for s in range(S):
                store(TURNS - 1, s)
            for s in range(S):
                sp.wait_ge(s_out[s], 16 + 16 * TURNS)

        @block.gpsimd
        def _(pool):
            pool.dma_start(rows_in[0:NB, :], b1.rearrange("l (f p) -> (l f) p", p=P)).then_inc(s_rows, 16)
            pool.dma_start(rows_in[NB:NB + NK, :], g1.rearrange("l (k p) -> (l k) p", p=P)).then_inc(s_rows, 16)
            pool.dma_start(rows_in[NB + NK:NB + 2 * NK, :], beta1.rearrange("l (k p) -> (l k) p", p=P))\
                .then_inc(s_rows, 16)
            pool.memset(ident[:, :], 0.0).then_inc(s_made, 1)
            pool.wait_ge(s_made, 1)
            pool.affine_select(out=ident[:, :], in_=ident[:, :], compare_op=ALU.not_equal, fill=1.0,
                               base=0, pattern=[[-1, P]], channel_multiplier=1).then_inc(s_made, 1)
            pool.memset(half_neg[:, :], -0.5).then_inc(s_made, 1)
            pool.memset(f32(G_hi[:, :]), 0.0).then_inc(s_made, 1)
            pool.memset(f32(sel[:, :, :]), 0.0).then_inc(s_made, 1)
            pool.memset(f32(dst_row[:, :]), 0.0).then_inc(s_made, 1)
            pool.memset(f32(xa_hi[:, :, D:D + 1]), 1.0).then_inc(s_made, 1)
            pool.memset(f32(xa_hi[:, :, D + 1:D + 2]), 0.0).then_inc(s_made, 1)
            pool.memset(f32(xa_lo[:, :, D:D + 2]), 0.0).then_inc(s_made, 1)
            pool.wait_ge(s_ready, 1)

            def masks(it, s):
                pool_waits(pool, s_adj, it * (16 * S) + 16 * (s + 1))
                pool.tensor_scalar(edge0[:, s, :, :], adj_in[:, :, :], 0.0, MASKED, ALU.is_le, ALU.mult)
                pool.tensor_scalar(edge1[:, s, :, :], adj_in[:, :, :], 1.0, None, ALU.mult)\
                    .then_inc(s_adj_used, 1)
                pool.wait_ge(s_adj_used, it * S + s + 1)
                pool.tensor_tensor(edge1[:, s, :, :], edge1[:, s, :, :],
                                   spread(ident[:, :].rearrange("p (o n) -> p o n", o=1), [P, G, N]),
                                   ALU.add).then_inc(s_self, 1)
                pool_waits(pool, s_self, it * S + s + 1)
                pool.tensor_scalar(edge1[:, s, :, :], edge1[:, s, :, :], 0.0, MASKED, ALU.is_le, ALU.mult)\
                    .then_inc(s_edges, 1)

            def add_source(it, q, src):
                pool.wait_ge(s_u, it * Q + q + 1)
                if q >= 2:
                    pool.wait_ge(s_pT, it * Q + q - 1)
                b = q % 2
                pool.tensor_tensor(w[:, b, :].rearrange("p (g n) -> p g n", g=G),
                                   u[:, b, :].rearrange("p (g n) -> p g n", g=G),
                                   spread(src.rearrange("p (g o) -> p g o", o=1), [P, G, N]),
                                   ALU.add).then_inc(s_src, 1)

            def inverse_root(it, kind, per, n):
                pool.wait_ge(s_eps[kind], it * per + n + 1)
                pool.tensor_tensor(rstd[kind][:, :], vareps[kind][:, :], half_neg[:, :], ALU.pow)\
                    .then_inc(s_rstd[kind], 1)

            def residual(it, n):
                l, s = n // S, n % S
                pool.wait_ge(s_nT, it * (SLOTS * KD) + (n + 1) * KD)
                for g in range(G):
                    pool.tensor_tensor(xs[:, s, g, :], xs[:, s, g, :], gamma1[:, l, :], ALU.mult).then_inc(s_hb_step, 1)
                    pool.wait_ge(s_hb_step, it * (SLOTS * G) + n * G + g + 1)
                    pool.tensor_tensor(xs[:, s, g, :], xs[:, s, g, :], shift1[:, l, :], ALU.add).then_inc(s_hb, 1)

            def affine(it, n):
                l, s = n // S, n % S
                for g in range(G):
                    if n + S < SLOTS:
                        pool.wait_ge(s_sd, it * (SLOTS * G) + (n + S) * G + g + 1)
                    else:
                        pool.wait_ge(s_norm["n2"], it * (SLOTS * G) + n * G + g + 1)
                    pool.tensor_tensor(xs[:, s, g, :], xs[:, s, g, :], gamma2[:, l, :], ALU.mult)\
                        .then_inc(s_aff_step, 1)
                    pool.wait_ge(s_aff_step, it * (SLOTS * G) + n * G + g + 1)
                    pool.tensor_tensor(xs[:, s, g, :], xs[:, s, g, :], shift2[:, l, :], ALU.add)\
                        .then_inc(s_aff, 1)

            with pool.Fori(0, TURNS) as it:
                for s in range(S):
                    masks(it, s)
                    for h in range(H):
                        add_source(it, s * H + h, src0[:, :, h])
                        if s and h == G + 1:
                            inverse_root(it, "l0", S, s - 1)
                inverse_root(it, "l0", S, S - 1)
                add_source(it, S * H, src1[:, :])
                inverse_root(it, "n1", SLOTS, 0)
                for n in range(SLOTS):
                    if n:
                        inverse_root(it, "n2", SLOTS, n - 1)
                        affine(it, n - 1)
                        if n - 1 >= SLOTS - S:
                            inverse_root(it, "end", S, n - 1 - (SLOTS - S))
                    if n + 1 < SLOTS:
                        add_source(it, S * H + n + 1, src1[:, :])
                    residual(it, n)
                    if n + 1 < SLOTS:
                        inverse_root(it, "n1", SLOTS, n + 1)
                inverse_root(it, "n2", SLOTS, SLOTS - 1)
                affine(it, SLOTS - 1)
                inverse_root(it, "end", S, S - 1)

        @block.scalar
        def _(act):
            act.dma_start(wp_in, w_proj.rearrange("(k p) d -> p k d", p=P)).then_inc(s_wp, 16)
            act.dma_start(watt_b, all_partitions(w_att.rearrange("h k -> (h k)"), H * K2)
                          .rearrange("p (h k) -> p h k", h=H)).then_inc(s_wp, 16)
            for dst, src, n in ((attw, attn_w, L * 2 * D), (gamma1, g1, L * D), (shift1, beta1, L * D),
                                (gamma2, g2, L * D), (shift2, beta2, L * D)):
                act.dma_start(dst[:, :, :].rearrange("p l d -> p (l d)"),
                              all_partitions(src.rearrange("l d -> (l d)"), n)).then_inc(s_consts, 16)
            act.dma_start(batt[:, :], all_partitions(b_att, H)).then_inc(s_consts, 16)
            act.dma_start(attb[:, :], all_partitions(attn_b, L)).then_inc(s_consts, 16)
            act.wait_ge(s_prep, 4 * KD)
            act.dma_start(b2_b.rearrange("p l d -> p (l d)"), all_partitions(b2.rearrange("l d -> (l d)"), L * D))\
               .then_inc(s_consts, 16)
            for b, (up, l, part) in enumerate(blocks):
                act.wait_ge(s_stage[b % 2], 16 * (b // 2 + 1))
                if up:
                    act.wait_ge(s_cols, 1)
                    c = NB + l * KD + part
                    act.activation(weight_dst(b, w1_hi, w2_hi), stage_flat(b), ACT.Identity,
                                   scale=cols[:, c:c + 1]).then_inc(s_hi_done, 1)
                else:
                    act.activation(weight_dst(b, w1_hi, w2_hi), stage_flat(b), ACT.Copy)\
                       .then_inc(s_hi_done, 1)

            def xT_hi(it, s):
                for k in range(KD):
                    act.wait_ge(s_xT, it * (S * KD) + s * KD + k + 1)
                    act.activation(nT_hi[:, k, :], [Z, T][k][:, :], ACT.Copy).then_inc(s_xT_hi, 1)

            def xh_parts(it, s):
                act.wait_ge(s_drow, it * S + s + 1)
                act.activation(dst_rows[0:H, :], U0[0:H, :], ACT.Copy).then_inc(s_drow_hi, 1)
                for g in range(G):
                    act.wait_ge(s_proj, it * (S * G) + s * G + g + 1)
                    act.activation(xh_hi[:, g, :, 0:KH],
                                   out0_bank[g][:, 0:D].rearrange("p (h c) -> p h c", h=H), ACT.Copy)\
                       .then_inc(s_xh_hi, 1)

            def exponential(it, q):
                act.wait_ge(s_leaky, it * Q + q + 1)
                b = q % 2
                for g in range(G):
                    c = slice(g * N, (g + 1) * N)
                    ins = act.activation(w[:, b, c], w[:, b, c], ACT.Exp, bias=neg_top[:, q % 4, g:g + 1])
                ins.then_inc(s_p, 1)

            def probsT_hi(it, q):
                act.wait_ge(s_pT, it * Q + q + 1)
                heads = q < S * H
                if heads and q % H >= 2:
                    act.wait_ge(s_head, it * (S * H) + q - 1)
                act.activation(pT0_hi[q % 2] if heads else nT_hi[:, 0, :],
                               pT_bank[q % 2 if heads else 0][:, :], ACT.Copy).then_inc(s_pT_hi, 1)

            def dstT_hi(it, n):
                act.wait_ge(s_dT, it * SLOTS + n + 1)
                act.activation(dst_row[0:G, :], T[0:G, 0:P], ACT.Copy).then_inc(s_dT_hi, 1)

            def nT_hi_parts(it, n):
                for k in range(KD):
                    act.wait_ge(s_nT, it * (SLOTS * KD) + n * KD + k + 1)
                    act.activation(nT_hi[:, k, :], [Z, T][k][:, :], ACT.Copy).then_inc(s_nT_hi, 1)

            def attention(it, n):
                q = S * H + n
                exponential(it, q)
                probsT_hi(it, q)
                nT_hi_parts(it, n)

            with act.Fori(0, TURNS) as it:
                for s in range(S):
                    xT_hi(it, s)
                    xh_parts(it, s)
                    for h in range(H + 1):
                        q = s * H + h
                        if h < H:
                            exponential(it, q)
                        if h:
                            probsT_hi(it, q - 1)
                dstT_hi(it, 0)
                attention(it, 0)
                for n in range(SLOTS):
                    l = n // S
                    for f in range(FT):
                        e = n * FT + f
                        act.wait_ge(s_up, it * (SLOTS * FT) + e + 1)
                        if e >= 2:
                            act.wait_ge(s_g_lo, it * (SLOTS * FT) + e - 1)
                        b = bias1[:, l * FT + f:l * FT + f + 1]
                        act.activation(g_full[:, f % 2, :], up_bank[f % 2][:, :], ACT.Gelu, bias=b)\
                           .then_inc(s_g, 1)
                        if f < HI_BY_ACT:
                            act.activation(Gh[:, f, :], up_bank[f % 2][:, :], ACT.Gelu, bias=b).then_inc(s_g_hi, 1)
                        if n + 1 < SLOTS and f == DST_AT:
                            dstT_hi(it, n + 1)
                    if n + 1 < SLOTS:
                        attention(it, n + 1)

        @block.tensor
        def _(pe):
            def split_matmul(dst, a_hi, a_lo, b_hi, b_lo, first, last):
                pe.matmul(dst, a_hi, b_hi, start=first, stop=False)
                pe.matmul(dst, a_hi, b_lo, start=False, stop=False)
                return pe.matmul(dst, a_lo, b_hi, start=False, stop=last)

            pe.wait_ge(s_made, 2)
            pe.wait_ge(s_rows, 48)
            nr = NB + 2 * NK
            pe.transpose(T[:, 0:nr], rows_in, ident[0:nr, 0:nr]).then_inc(s_cols_ps, 1)
            pe.wait_ge(s_cols, 1)
            done = 0
            for b, (up, l, part) in enumerate(blocks):
                if not up:
                    continue
                pe.wait_ge(s_stage[b % 2], 16 * (b // 2 + 1))
                c = NB + NK + l * KD + part
                for f in range(FT):
                    mm = pe.matmul([Z, U0][part][:, l * FT + f:l * FT + f + 1],
                                   stage_flat(b)[:, f * P:(f + 1) * P], cols[:, c:c + 1], start=True, stop=True)
                mm.then_inc(s_bmm, 1)
            pe.wait_ge(s_ready, 1)

            def transposes_to(banks, src, done_sem, waits=None):
                for k in range(KD):
                    for g in range(G):
                        if waits is not None and k == 0:
                            pe.wait_ge(*waits(g))
                        t = pe.transpose(banks[k][:, g * P:(g + 1) * P], src[:, g, k * P:(k + 1) * P], ident[:, :])
                    t.then_inc(done_sem, 1)

            def project(it, s):
                pe.wait_ge(s_x[s], it * 16 + 16)
                transposes_to([Z, T], x0[:, s, :, :], s_xT)
                pe.wait_ge(s_xT_lo, it * (S * KD) + (s + 1) * KD)
                for k in range(KD):
                    mm = split_matmul(U0[0:H, :], wp_hi[:, k, D + H:PW], wp_lo[:, k, D + H:PW],
                                      nT_hi[:, k, :], nT_lo[:, k, :], k == 0, k == KD - 1)
                mm.then_inc(s_drow, 1)
                if s == 0:
                    pe.wait_ge(s_sum["n2"], it * (SLOTS * G) + 1)
                for g in range(G):
                    if s:
                        pe.wait_ge(s_scaled, it * (S * G) + (s - 1) * G + g + 1)
                    c = slice(g * P, (g + 1) * P)
                    for k in range(KD):
                        mm = split_matmul(out0_bank[g][:, 0:D + H], nT_hi[:, k, c], nT_lo[:, k, c],
                                          wp_hi[:, k, 0:D + H], wp_lo[:, k, 0:D + H], k == 0, k == KD - 1)
                    mm.then_inc(s_proj, 1)

            def head_scores(it, s, h):
                if h == 0:
                    pe.wait_ge(s_drow_lo, it * S + s + 1)
                if h >= 2:
                    pe.wait_ge(s_u, it * Q + s * H + h - 1)
                pe.matmul(z_bank[h % 2][:, :], sel[:, h, :], dst_rows, start=True, stop=True).then_inc(s_z, 1)

            def turn_probs(it, q, dst):
                pe.wait_ge(s_p, it * Q + q + 1)
                if q % H >= 2 and q < S * H:
                    pe.wait_ge(s_pT_lo, it * Q + q - 1)
                for g in range(G):
                    t = pe.transpose(dst[:, g * P:(g + 1) * P], w[:, q % 2, g * P:(g + 1) * P], ident[:, :])
                t.then_inc(s_pT, 1)

            def head_sum(it, s, h):
                q = s * H + h
                if h == 0:
                    pe.wait_ge(s_xh_lo, it * (S * G) + (s + 1) * G)
                pe.wait_ge(s_pT_lo, it * Q + q + 1)
                for g in range(G):
                    c = slice(g * P, (g + 1) * P)
                    mm = split_matmul(out0_bank[g][:, h * HW:(h + 1) * HW], pT0_hi[h % 2][:, c], pT0_lo[h % 2][:, c],
                                      xh_hi[:, g, h, :], xh_lo[:, g, h, :], True, True)
                mm.then_inc(s_head, 1)

            def turn_dst(it, n):
                pe.wait_ge(s_sd, it * (SLOTS * G) + (n + 1) * G)
                pe.transpose(T[0:G, 0:P], dst1[:, :], ident[:, :]).then_inc(s_dT, 1)

            def dst_scores(it, n):
                pe.wait_ge(s_dT_lo, it * SLOTS + n + 1)
                for g in range(G):
                    mm = pe.matmul(Z[:, g * P:(g + 1) * P], sel[0:32 + G, g, :], dst_row[0:32 + G, :],
                                   start=True, stop=True)
                mm.then_inc(s_z, 1)

            def aggregate(it, n, graphs):
                q = S * H + n
                for g in graphs:
                    if g == 0:
                        pe.wait_ge(s_xa_lo, it * SLOTS + n + 1)
                        pe.wait_ge(s_pT_lo, it * Q + q + 1)
                    if g >= 2:
                        pe.wait_ge(s_sum["n1"], it * (SLOTS * G) + n * G + g - 1)
                    c = slice(g * P, (g + 1) * P)
                    split_matmul(agg_bank[g % 2][:, 0:XW], nT_hi[:, 0, c], nT_lo[:, 0, c],
                                 xa_hi[:, g, :], xa_lo[:, g, :], True, True).then_inc(s_agg, 1)

            def turn_norm(it, n):
                transposes_to([Z, T], xs[:, n % S, :, :], s_nT,
                              lambda g: (s_norm["n1"], it * (SLOTS * G) + n * G + g + 1))

            def up(it, n, f):
                l = n // S
                e = n * FT + f
                c = slice(f * P, (f + 1) * P)
                if f == 0:
                    pe.wait_ge(s_nT_lo, it * (SLOTS * KD) + n * KD + 1)
                if e >= 2:
                    pe.wait_ge(s_g_hi, it * (SLOTS * FT) + e - 1)
                for k in range(KD):
                    if f == 0 and k == KD - 1:
                        pe.wait_ge(s_nT_lo, it * (SLOTS * KD) + (n + 1) * KD)
                    mm = split_matmul(up_bank[f % 2][:, :], w1_hi[:, l, k, c], w1_lo[:, l, k, c],
                                      nT_hi[:, k, :], nT_lo[:, k, :], k == 0, k == KD - 1)
                mm.then_inc(s_up, 1)

            def down(it, n, g, part):
                l = n // S
                c = slice(g * P, (g + 1) * P)
                e = n * G + g
                if part == 0:
                    if e < 2:
                        pe.wait_ge(s_scaled, it * (S * G) + S * G)
                    else:
                        pe.wait_ge(s_sum["n2"], it * (SLOTS * G) + 1 + e - 1)
                for f in range(part * HF, (part + 1) * HF):
                    if g == 0:
                        pe.wait_ge(s_g_lo, it * (SLOTS * FT) + n * FT + f + 1)
                    mm = split_matmul(down_bank[g % 2][:, 0:D], Gh[:, f, c], Gl[:, f, c],
                                      w2_hi[:, l, f, :], w2_lo[:, l, f, :], f == 0, f == FT - 1)
                if part:
                    mm.then_inc(s_down, 1)

            with pe.Fori(0, TURNS) as it:
                for s in range(S):
                    project(it, s)
                    head_scores(it, s, 0)
                    head_scores(it, s, 1)
                    for h in range(H + 2):
                        if h + 2 < H:
                            head_scores(it, s, h + 2)
                        if h < H:
                            turn_probs(it, s * H + h, pT_bank[h % 2])
                        if h >= 2:
                            head_sum(it, s, h - 2)
                turn_dst(it, 0)
                dst_scores(it, 0)
                turn_probs(it, S * H, T)
                aggregate(it, 0, range(G))
                turn_norm(it, 0)
                for n in range(SLOTS):
                    m = n + 1
                    more = m < SLOTS
                    for f in range(FT):
                        up(it, n, f)
                        if more and f == DST_AT:
                            turn_dst(it, m)
                        if more and f == SCORES_AT:
                            dst_scores(it, m)
                    down(it, n, 0, 0)
                    down(it, n, 0, 1)
                    down(it, n, 1, 0)
                    if more:
                        turn_probs(it, S * H + m, T)
                    down(it, n, 1, 1)
                    if more:
                        aggregate(it, m, range(0, 2))
                    down(it, n, 2, 0)
                    if more:
                        aggregate(it, m, range(2, G))
                    down(it, n, 2, 1)
                    down(it, n, 3, 0)
                    down(it, n, 3, 1)
                    if more:
                        turn_norm(it, m)

        @block.vector
        def _(dve):
            steps = [0]

            def prep(ins):
                steps[0] += 1
                ins.then_inc(s_prep, 1)
                dve.wait_ge(s_prep, steps[0])

            dve.wait_ge(s_wp, 32)
            for k in range(KD):
                for side in range(2):
                    prep(dve.tensor_tensor(prod.rearrange("p (h c) -> p h c", h=H),
                                           wp_in[:, k, :].rearrange("p (h c) -> p h c", h=H),
                                           watt_b[:, :, side * KH:(side + 1) * KH], ALU.mult))
                    prep(dve.tensor_reduce(wsum[:, k, side * H:(side + 1) * H],
                                           prod.rearrange("p (h c) -> p h c", h=H), AX_X, ALU.add))
            for part, src in ((slice(0, D), wp_in), (slice(D, PW), wsum)):
                prep(dve.tensor_copy(wp_hi[:, :, part], src))
                prep(dve.tensor_tensor(wp_lo[:, :, part], src, f32(wp_hi[:, :, part]), ALU.subtract))
            dve.wait_ge(s_cols_ps, 1)
            dve.tensor_copy(cols[:, :], T[:, 0:NB + 2 * NK]).then_inc(s_cols, 1)
            dve.wait_ge(s_made, 9)
            for first in (0, 32):
                some = slice(first, first + H)
                prep(dve.tensor_copy(sel[some, :, :],
                                     spread(ident[some, some].rearrange("p (h o) -> p h o", o=1), [H, H, P])))
            dve.wait_ge(s_cols, 1)
            n_up = 0
            for b, (is_up, l, part) in enumerate(blocks):
                dve.wait_ge(s_hi_done, b + 1)
                hi, lo = weight_dst(b, w1_hi, w2_hi), weight_dst(b, w1_lo, w2_lo)
                if is_up:
                    n_up += 1
                    dve.wait_ge(s_bmm, n_up)
                    c = NB + l * KD + part
                    dve.scalar_tensor_tensor(lo, stage_flat(b), cols[:, c:c + 1], f32(hi),
                                             ALU.mult, ALU.subtract).then_inc(s_lo_done, 1)
                else:
                    dve.tensor_tensor(lo, stage_flat(b), f32(hi), ALU.subtract).then_inc(s_lo_done, 1)
            prep(dve.tensor_tensor(bias1_part[:, :], Z[:, 0:NB], cols[:, 0:NB], ALU.add))
            prep(dve.tensor_tensor(bias1[:, :], U0[:, 0:NB], bias1_part[:, :], ALU.add))
            dve.wait_ge(s_consts, 16 * 8)
            prep(dve.tensor_tensor(shift1[:, :, :], shift1[:, :, :], b2_b, ALU.add))
            for l in range(1, L):
                for side in range(2):
                    prep(dve.tensor_tensor_reduce(
                        out=prod, in0=attw[:, l, side * D:(side + 1) * D], in1=shift2[:, l - 1, :], scale=1.0,
                        scalar=attb[:, l:l + 1], op0=ALU.mult, op1=ALU.add, accum_out=recip1[:, 0:1]))
                    prep(dve.tensor_copy(attb[:, l:l + 1], recip1[:, 0:1]))
                    prep(dve.tensor_tensor(attw[:, l, side * D:(side + 1) * D],
                                           attw[:, l, side * D:(side + 1) * D], gamma2[:, l - 1, :], ALU.mult))
            dve.tensor_copy(recip1[:, 0:1], attb[:, 0:1]).then_inc(s_sum["n2"], 1)
            for s in range(S):
                dve.tensor_copy(recip1[:, 1 + s:2 + s], attb[:, 0:1]).then_inc(s_out[s], 16)
            dve.tensor_copy(recip1[:, 3:4], attb[:, 0:1]).then_inc(s_ready, 1)

            def low_part(dst, src, hi):
                return dve.tensor_tensor(dst, src, f32(hi), ALU.subtract)

            def xT_lo(it, s):
                for k in range(KD):
                    dve.wait_ge(s_xT_hi, it * (S * KD) + s * KD + k + 1)
                    low_part(nT_lo[:, k, :], [Z, T][k][:, :], nT_hi[:, k, :]).then_inc(s_xT_lo, 1)

            def xh_parts(it, s):
                dve.wait_ge(s_drow_hi, it * S + s + 1)
                if s == 0:
                    dve.memset(f32(xh_hi[:, :, :, KH:KH + 1]), 1.0)
                    dve.memset(f32(xh_hi[:, :, :, KH + 1:HW]), 0.0)
                    dve.memset(f32(xh_lo[:, :, :, KH:HW]), 0.0)
                low_part(dst_rows[32:32 + H, :], U0[0:H, :], dst_rows[0:H, :]).then_inc(s_drow_lo, 1)
                for g in range(G):
                    dve.wait_ge(s_xh_hi, it * (S * G) + s * G + g + 1)
                    low_part(xh_lo[:, g, :, 0:KH], out0_bank[g][:, 0:D].rearrange("p (h c) -> p h c", h=H),
                             xh_hi[:, g, :, 0:KH])
                    dve.tensor_tensor(src0[:, g, :], out0_bank[g][:, D:D + H], batt[:, :], ALU.add)\
                       .then_inc(s_xh_lo, 1)

            def masked_scores(it, q, bank_, edge, src):
                b = q % 2
                if q >= 2:
                    dve.wait_ge(s_src, it * Q + q - 1)
                vector_waits(dve, s_z, it * Q + q + 1)
                for g in range(G):
                    ins = dve.tensor_tensor_reduce(
                        out=u[:, b, g * N:(g + 1) * N], in0=bank_[:, g * N:(g + 1) * N], in1=edge[:, g, :],
                        scale=1.0, scalar=-3.0e38, op0=ALU.add, op1=ALU.max, accum_out=row_max[:, g:g + 1])
                ins.then_inc(s_u, 1)
                dve.wait_ge(s_u, it * Q + q + 1)
                dve.scalar_tensor_tensor(neg_z[:, :], row_max[:, :], -1.0, src, ALU.mult, ALU.subtract)\
                   .then_inc(s_neg_z, 1)
                dve.wait_ge(s_neg_z, it * Q + q + 1)
                dve.scalar_tensor_tensor(neg_top[:, q % 4, :], neg_z[:, :], SLOPE, neg_z[:, :], ALU.mult, ALU.min)

            def leaky(it, q):
                dve.wait_ge(s_src, it * Q + q + 1)
                dve.scalar_tensor_tensor(w[:, q % 2, :], w[:, q % 2, :], SLOPE, w[:, q % 2, :],
                                         ALU.mult, ALU.max).then_inc(s_leaky, 1)

            def probsT_lo(it, q):
                heads = q < S * H
                dve.wait_ge(s_pT_hi, it * Q + q + 1)
                low_part(pT0_lo[q % 2] if heads else nT_lo[:, 0, :], pT_bank[q % 2 if heads else 0][:, :],
                         pT0_hi[q % 2] if heads else nT_hi[:, 0, :]).then_inc(s_pT_lo, 1)

            def row_stats(it, kind, per, n, g, rows):
                e = it * (per * G) + n * G + g + (1 if kind == "n2" else 0)
                dve.wait_ge(s_sum[kind], e + 1)
                dve.bn_stats(stats[kind][:, g, :], rows).then_inc(s_stat[kind], 1)

            def mean_var(it, kind, per, n):
                for g in range(G):
                    if g == 0:
                        vector_waits(dve, s_stat[kind], it * (per * G) + (n + 1) * G)
                    ins = dve.bn_aggr(meanvar[kind][:, g, :], stats[kind][:, g, :])
                ins.then_inc(s_var[kind], 1)
                dve.wait_ge(s_var[kind], it * per + n + 1)
                dve.tensor_scalar(vareps[kind][:, :], meanvar[kind][:, :, 1], EPS, None, ALU.add)\
                   .then_inc(s_eps[kind], 1)

            def normalize(it, kind, per, n, g, dst, rows):
                if g == 0:
                    dve.wait_ge(s_rstd[kind], it * per + n + 1)
                dve.tensor_scalar(dst, rows, meanvar[kind][:, g, 0:1], rstd[kind][:, g:g + 1],
                                  ALU.subtract, ALU.mult).then_inc(s_norm[kind], 1)

            SD_FIRST = 2
            RN = (S + SLOTS) * G

            def heads_take(it, s):
                dve.wait_ge(s_head, it * (S * H) + (s + 1) * H)
                dve.wait_ge(s_out[s], it * 16 + 16)
                heads = [b[:, 0:H * HW].rearrange("p (h c) -> p h c", h=H) for b in out0_bank]
                for g in range(G):
                    dve.reciprocal(recip0[:, g, :], heads[g][:, :, KH]).then_inc(s_recip, 1)
                for g in range(G):
                    dve.wait_ge(s_recip, it * RN + s * G + g + 1)
                    dve.tensor_tensor(xs[:, s, g, :].rearrange("p (h c) -> p h c", h=H), heads[g][:, :, 0:KH],
                                      spread(recip0[:, g, :].rearrange("p (h o) -> p h o", o=1), [P, H, KH]),
                                      ALU.mult).then_inc(s_scaled, 1)

            def heads_sum(it, s, g):
                rows = xs[:, s, g, :]
                dve.wait_ge(s_scaled, it * (S * G) + s * G + g + 1)
                dve.scalar_tensor_tensor(rows, rows, 0.0, x0[:, s, g, :], ALU.max, ALU.add)\
                   .then_inc(s_sum["l0"], 1)

            def heads_norm(it, s):
                for g in range(G):
                    normalize(it, "l0", S, s, g, x0[:, s, g, :], xs[:, s, g, :])

            def gelu_parts(it, n, f):
                e = it * (SLOTS * FT) + n * FT + f + 1
                if f >= HI_BY_ACT:
                    dve.wait_ge(s_g, e)
                    dve.tensor_copy(Gh[:, f, :], g_full[:, f % 2, :]).then_inc(s_g_hi, 1)
                dve.wait_ge(s_g_hi, e)
                low_part(Gl[:, f, :], g_full[:, f % 2, :], Gh[:, f, :]).then_inc(s_g_lo, 1)

            def src_dst(it, n, g):
                l, s = n // S, n % S
                rows = (x0 if l == 0 else xs)[:, s, g, :]
                if l == 0:
                    dve.wait_ge(s_norm["l0"], it * (S * G) + s * G + g + 1)
                else:
                    dve.wait_ge(s_norm["n2"], it * (SLOTS * G) + (n - S) * G + g + 1)
                if g:
                    dve.wait_ge(s_sd, it * (SLOTS * G) + n * G + g)
                junk, junk2 = (w[:, (n + 1) % 2, i * D:(i + 1) * D] for i in range(2))
                dve.tensor_tensor_reduce(out=junk, in0=rows, in1=attw[:, l, 0:D], scale=1.0,
                                         scalar=attb[:, l:l + 1], op0=ALU.mult, op1=ALU.add,
                                         accum_out=src1[:, g:g + 1])
                dve.tensor_tensor_reduce(out=junk2, in0=rows, in1=attw[:, l, D:2 * D], scale=1.0,
                                         scalar=0.0, op0=ALU.mult, op1=ALU.add,
                                         accum_out=dst1[:, g:g + 1]).then_inc(s_sd, 1)

            def xa_parts(it, n):
                l, s = n // S, n % S
                src = (x0 if l == 0 else xs)[:, s, :, :]
                if l == 0:
                    dve.wait_ge(s_norm["l0"], it * (S * G) + (s + 1) * G)
                else:
                    dve.wait_ge(s_aff, it * (SLOTS * G) + (n - S + 1) * G)
                if n:
                    dve.wait_ge(s_agg, it * (SLOTS * G) + n * G)
                dve.tensor_copy(xa_hi[:, :, 0:D], src).then_inc(s_xa_hi, 1)
                dve.wait_ge(s_xa_hi, it * SLOTS + n + 1)
                low_part(xa_lo[:, :, 0:D], src, xa_hi[:, :, 0:D]).then_inc(s_xa_lo, 1)

            def dstT_lo(it, n):
                dve.wait_ge(s_dT_hi, it * SLOTS + n + 1)
                low_part(dst_row[32:32 + G, :], T[0:G, 0:P], dst_row[0:G, :]).then_inc(s_dT_lo, 1)

            def attention_sums(it, n, graphs):
                l, s = n // S, n % S
                for g in graphs:
                    dve.wait_ge(s_agg, it * (SLOTS * G) + n * G + g + 1)
                    dve.reciprocal(recip1[:, g:g + 1], agg_bank[g % 2][:, D:D + 1]).then_inc(s_recip, 1)
                for g in graphs:
                    dve.wait_ge(s_recip, it * RN + (S + n) * G + g + 1)
                    dve.scalar_tensor_tensor(xs[:, s, g, :], agg_bank[g % 2][:, 0:D], recip1[:, g:g + 1],
                                             (x0 if l == 0 else xs)[:, s, g, :], ALU.mult, ALU.add)\
                       .then_inc(s_sum["n1"], 1)
                for g in graphs:
                    row_stats(it, "n1", SLOTS, n, g, xs[:, s, g, :])

            def attention_norm(it, n):
                for g in range(G):
                    normalize(it, "n1", SLOTS, n, g, xs[:, n % S, g, :], xs[:, n % S, g, :])

            def nT_lo_parts(it, n):
                for k in range(KD):
                    dve.wait_ge(s_nT_hi, it * (SLOTS * KD) + n * KD + k + 1)
                    low_part(nT_lo[:, k, :], [Z, T][k][:, :], nT_hi[:, k, :]).then_inc(s_nT_lo, 1)

            def feed_forward_sum(it, n, g):
                s = n % S
                dve.wait_ge(s_down, it * (SLOTS * G) + n * G + g + 1)
                dve.wait_ge(s_hb, it * (SLOTS * G) + n * G + g + 1)
                dve.tensor_tensor(xs[:, s, g, :], down_bank[g % 2][:, 0:D], xs[:, s, g, :], ALU.add)\
                   .then_inc(s_sum["n2"], 1)

            def feed_forward_norm(it, n):
                for g in range(G):
                    normalize(it, "n2", SLOTS, n, g, xs[:, n % S, g, :], xs[:, n % S, g, :])

            def end_sum(it, s, g):
                dve.wait_ge(s_aff, it * (SLOTS * G) + (SLOTS - S + s) * G + g + 1)
                dve.tensor_tensor(xs[:, s, g, :], xs[:, s, g, :], x0[:, s, g, :], ALU.add)\
                   .then_inc(s_sum["end"], 1)
                row_stats(it, "end", S, s, g, xs[:, s, g, :])

            def end_norm(it, s):
                for g in range(G):
                    normalize(it, "end", S, s, g, xs[:, s, g, :], xs[:, s, g, :])

            def rows_of(s, g):
                return xs[:, s, g, :]

            with dve.Fori(0, TURNS) as it:
                for s in range(S):
                    xT_lo(it, s)
                    xh_parts(it, s)
                    vector_waits(dve, s_edges, it * S + s + 1)
                    masked_scores(it, s * H, z_bank[0], edge0[:, s, :, :], src0[:, :, 0])
                    for h in range(H + 2):
                        if h + 1 < H:
                            masked_scores(it, s * H + h + 1, z_bank[(h + 1) % 2], edge0[:, s, :, :],
                                          src0[:, :, h + 1])
                        if h < H:
                            leaky(it, s * H + h)
                        if h >= 2:
                            probsT_lo(it, s * H + h - 2)
                        if s and 1 <= h <= G:
                            heads_sum(it, s - 1, h - 1)
                            row_stats(it, "l0", S, s - 1, h - 1, rows_of(s - 1, h - 1))
                        if s and h == G:
                            mean_var(it, "l0", S, s - 1)
                        if s and h == G + 2:
                            heads_norm(it, s - 1)
                    heads_take(it, s)
                for g in range(G):
                    src_dst(it, 0, g)
                for g in range(G):
                    heads_sum(it, S - 1, g)
                    row_stats(it, "l0", S, S - 1, g, rows_of(S - 1, g))
                mean_var(it, "l0", S, S - 1)
                for n in range(-1, SLOTS):
                    m = n + 1
                    if n >= 0:
                        last = n - 1 >= SLOTS - S
                        if n:
                            feed_forward_norm(it, n - 1)
                        else:
                            heads_norm(it, S - 1)
                        for f in range(FT):
                            if m < SLOTS and f == 0:
                                for g in range(SD_FIRST):
                                    src_dst(it, m, g)
                            gelu_parts(it, n, f)
                            if m < SLOTS and SD_FIRST <= f + SD_FIRST < G:
                                src_dst(it, m, f + SD_FIRST)
                            if m < SLOTS and f == DST_AT:
                                dstT_lo(it, m)
                            if m < SLOTS and f == SCORES_AT:
                                masked_scores(it, S * H + m, Z, edge1[:, m % S, :, :], src1[:, :])
                            if m < SLOTS and f == SCORES_AT + 1:
                                leaky(it, S * H + m)
                            if last and 2 <= f < 2 + G:
                                end_sum(it, n - 1 - (SLOTS - S), f - 2)
                        if last:
                            mean_var(it, "end", S, n - 1 - (SLOTS - S))
                    elif m < SLOTS:
                        dstT_lo(it, m)
                        masked_scores(it, S * H + m, Z, edge1[:, m % S, :, :], src1[:, :])
                        leaky(it, S * H + m)
                    if m < SLOTS:
                        xa_parts(it, m)
                    if n >= 0:
                        feed_forward_sum(it, n, 0)
                    if m < SLOTS:
                        probsT_lo(it, S * H + m)
                    if n >= 0:
                        row_stats(it, "n2", SLOTS, n, 0, rows_of(n % S, 0))
                        if n - 1 >= SLOTS - S:
                            end_norm(it, n - 1 - (SLOTS - S))
                        feed_forward_sum(it, n, 1)
                    if m < SLOTS:
                        attention_sums(it, m, range(0, 2))
                    if n >= 0:
                        row_stats(it, "n2", SLOTS, n, 1, rows_of(n % S, 1))
                    if m < SLOTS:
                        attention_sums(it, m, range(2, G))
                        mean_var(it, "n1", SLOTS, m)
                    if n >= 0:
                        feed_forward_sum(it, n, 2)
                        row_stats(it, "n2", SLOTS, n, 2, rows_of(n % S, 2))
                    if m < SLOTS:
                        attention_norm(it, m)
                    if n >= 0:
                        feed_forward_sum(it, n, 3)
                        row_stats(it, "n2", SLOTS, n, 3, rows_of(n % S, 3))
                    if m < SLOTS:
                        nT_lo_parts(it, m)
                    if n >= 0:
                        mean_var(it, "n2", SLOTS, n)
                feed_forward_norm(it, SLOTS - 1)
                for g in range(G):
                    end_sum(it, S - 1, g)
                mean_var(it, "end", S, S - 1)
                end_norm(it, S - 1)


_INS = ['x', 'adj', 'L0_gnn_W_proj', 'L0_gnn_W_att', 'L0_gnn_b_att', 'L1_gnn_attn_w', 'L1_gnn_attn_b',
        'L1_gnn_W1', 'L1_gnn_b1', 'L1_gnn_W2', 'L1_gnn_b2', 'L1_gnn_g1', 'L1_gnn_beta1', 'L1_gnn_g2',
        'L1_gnn_beta2']
_OUTS = [((64, 128, 256), 'float32')]


def kernel(**inputs):
    import numpy as _np
    import concourse.bacc as _bacc
    from concourse import mybir as _mybir
    from concourse.bass_utils import run_bass_kernel_spmd as _run

    nc = _bacc.Bacc("TRN2", target_bir_lowering=False, num_devices=1)
    arrays, args = {}, []
    for name in _INS:
        a = _np.ascontiguousarray(inputs[name])
        arrays[f"in_{name}_dram"] = a
        args.append(nc.dram_tensor(f"in_{name}_dram", a.shape, _mybir.dt.from_np(a.dtype),
                                   kind="ExternalInput").ap())
    for i, (shape, dtype) in enumerate(_OUTS):
        dt = _mybir.dt.from_np(_np.dtype(dtype))
        args.append(nc.dram_tensor(f"out_{i}_dram", shape, dt, kind="ExternalOutput").ap())
    graph_network(nc, *args)
    r = _run(nc, [arrays], core_ids=[0])
    return r.results[0]["out_0_dram"]
```

```python
from contextlib import ExitStack
from itertools import cycle

import concourse.bass as bass
from concourse import mybir

F32 = mybir.dt.float32
F32R = mybir.dt.float32r
BF16 = mybir.dt.bfloat16
I32 = mybir.dt.int32
ALU = mybir.AluOpType
ACT = mybir.ActivationFunctionType
AX_X = mybir.AxisListType.X

EPS = 1e-5
SLOPE = 0.2
MASKED = -(2.0 ** 100)


def graph_network(nc, x, adj, w_proj, w_att, b_att, attn_w, attn_b, W1, b1, W2, b2,
                  g1, beta1, g2, beta2, out):
    B, N, D = x.shape
    H, K2 = w_att.shape
    KH = K2 // 2
    L = attn_w.shape[0]
    F = W1.shape[2]
    P = N
    G = 4
    S = 2
    TURNS = B // (G * S)
    KD = D // P
    FT = F // P
    NG = G * N
    assert P == 128 and NG == 512 and H * KH == D and KD == 2

    SLOTS = S * L
    HF = FT // 2
    R = 2
    assert (SLOTS * FT) % R == 0

    SD_AT, PROBS_AT, SUM_AT, SUM2_AT = 2, 5, 6, 6
    KEEP_AT = 6
    END_AT = 3

    SPAN = 3 * FT
    X_AT = [g for g in range(G)]
    SCORE_AT = [5, 8, 9, 10, 12, 16, 17, 18]
    EXP_AT = [FT - 1] + 4 * [2 * FT - 1] + 3 * [2 * FT + PROBS_AT]
    TURN_AT = [8, 15, 16, 17, 18, 21, 22, 23]
    TAKE_AT = [TURN_AT[2 * p + 1] + 2 for p in range(H // 2)]
    bank_uses = sorted([(at, "x", g) for g, at in enumerate(X_AT)] +
                       [(at, "probs", h) for h, at in enumerate(TURN_AT)])
    USES = len(bank_uses)
    LATE = 2
    assert max(TAKE_AT) < SPAN + LATE and H == 8
    use_index = {(kind, i): j for j, (_, kind, i) in enumerate(bank_uses)}

    with ExitStack() as ctx:
        def sb(name, shape, dt=F32):
            return ctx.enter_context(nc.sbuf_tensor(name, shape, dt))

        def sem(name):
            return ctx.enter_context(nc.semaphore(name))

        w1_hi, w1_lo = (sb(f"w1_{p}", [P, L, KD, F], F32R) for p in ("hi", "lo"))
        w2_hi, w2_lo = (sb(f"w2_{p}", [P, L, FT, D], F32R) for p in ("hi", "lo"))
        PW = D + 2 * H
        wp_hi, wp_lo = (sb(f"wp_{p}", [P, KD, PW], F32R) for p in ("hi", "lo"))
        attw = sb("attw", [P, L, 2 * D])
        gamma1 = sb("gamma1", [P, L, D])
        shift1 = sb("shift1", [P, L, D])
        gamma2 = sb("gamma2", [P, L, D])
        shift2 = sb("shift2", [P, L, D])
        NB, NK = L * FT, L * KD
        cols = sb("cols", [P, NB + 2 * NK])
        bias1 = sb("bias1", [P, NB])
        bias1_part = sb("bias1_part", [P, NB])
        batt = sb("batt", [2 * H, 1])
        attb = sb("attb", [P, L])
        ident = sb("ident", [P, P])
        off_diag = sb("off_diag", [P, P], BF16)
        sel = sb("sel", [32 + 2 * H, 2 * H], F32R)
        half_neg = sb("half_neg", [P, G])

        MARKS = 16
        dve_mark = sb("dve_mark", [P, MARKS])
        pool_mark = sb("pool_mark", [P, MARKS])
        dve_marks, pool_marks = (cycle([slice(i, i + 1) for i in range(MARKS)]) for _ in range(2))

        xin = sb("xin", [P, S, G, D])
        x0 = sb("x0", [P, S, G, D])
        xs = sb("xs", [P, S, G, D])
        final = sb("final", [P, G, D])
        adj_in = sb("adj_in", [P, G, N], I32)
        edge0 = sb("edge0", [P, S, G, N], BF16)
        edge1 = sb("edge1", [P, S, G, N], BF16)
        xa_hi, xa_lo = (sb(f"xa_{p}", [P, G, D], F32R) for p in ("hi", "lo"))
        nT_hi, nT_lo = (sb(f"nT_{p}", [P, KD, NG], F32R) for p in ("hi", "lo"))
        G_hi, G_lo = (sb(f"G_{p}", [P, R, NG], F32R) for p in ("hi", "lo"))
        g_full = sb("g_full", [P, 2, NG])
        xh_hi, xh_lo = (sb(f"xh_{p}", [P, G, D], F32R) for p in ("hi", "lo"))
        rows0 = sb("rows0", [32 + 2 * H, NG], F32R)
        hT_hi, hT_lo = (sb(f"hT_{p}", [P, NG], F32R) for p in ("hi", "lo"))
        w0 = sb("w0", [P, 4, NG])
        w1 = sb("w1", [P, NG])
        sd = sb("sd", [P, 2 * G])
        rows1 = sb("rows1", [32 + 2 * G, P], F32R)
        top0 = sb("top0", [P, 4, G])
        top1 = sb("top1", [P, G])
        row_max0, row_max1, neg_max0, neg_max1 = (sb(k, [P, G]) for k in
                                                  ("row_max0", "row_max1", "neg_max0", "neg_max1"))
        sums0 = sb("sums0", [P, H // 2, G, 2])
        sums1 = sb("sums1", [P, G])
        recip0 = sb("recip0", [P, G, 2])
        recip1 = sb("recip1", [P, G])
        NORMS = ("l0", "n1", "n2", "end")
        stats = {k: sb(f"stats_{k}", [P, G, 6]) for k in NORMS}
        meanvar = {k: sb(f"meanvar_{k}", [P, G, 2]) for k in NORMS}
        vareps = {k: sb(f"vareps_{k}", [P, G]) for k in NORMS}
        rstd = {k: sb(f"rstd_{k}", [P, G]) for k in NORMS}

        stage = [g_full[:, :, :].rearrange("p a n -> p (a n)"), final[:, :, :].rearrange("p g d -> p (g d)")]
        watt_b = xs[:, 0, 0:2, :].rearrange("p a b -> p (a b)")[:, 0:H * K2].rearrange("p (h k) -> p h k", h=H)
        prod = xs[:, 1, 0, :]
        wp_in = x0[:, 0, 0:KD, :]
        wsum = x0[:, 1, 0:KD, 0:2 * H]
        rows_in = xs[0:NB + 2 * NK, 1, 1, 0:P]
        b2_b = xs[:, 0, 0:L, :]

        bank = [ctx.enter_context(nc.psum_tensor(f"bank{i}", [P, 512], F32)) for i in range(8)]
        U0, U1, V0, V1, Z, T, HB, HO = bank
        up_bank = [U0, U1]
        down_bank = [V0, V0, V1, V1]
        agg_bank = [Z, Z, T, T]

        WEIGHTS_AT = [2, 6]
        assert len(WEIGHTS_AT) * SLOTS == L * (KD + 2)
        HI_BY_ACT = 7
        FILL = 10

        def half(bank_, g):
            return bank_[:, (g % 2) * D:(g % 2) * D + D]

        s_rows = sem("rows_loaded")
        s_consts = sem("consts_loaded")
        s_batt = sem("head_bias_loaded")
        s_wp = sem("proj_loaded")
        s_stage = [sem(f"stage_loaded{i}") for i in range(2)]
        s_made = sem("pool_consts_made")
        s_prep = sem("prep_step")
        s_cols_ps = sem("columns_turned")
        s_cols = sem("columns_ready")
        s_bmm = sem("beta_product_done")
        s_hi_done = sem("weight_hi_done")
        s_lo_done = sem("weight_lo_done")
        s_bias = sem("bias_ready")
        s_ready = sem("weights_ready")
        s_x = [sem(f"x_loaded{s}") for s in range(S)]
        s_adj = sem("adj_loaded")
        s_edge0 = sem("edges_ready")
        s_edge1 = sem("self_edges_ready")
        s_hb = sem("heads_bank_filled")
        s_hb_read = sem("heads_bank_read")
        s_xT_hi = sem("xT_hi")
        s_proj = sem("projected")
        s_xh_hi = sem("xh_hi")
        s_xh_lo = sem("xh_lo")
        s_h_z = sem("head_scores_ready")
        s_h_max = sem("head_max")
        s_h_neg = sem("head_neg_max")
        s_h_w = sem("head_exponents")
        s_h_p = sem("head_probs")
        s_hT_hi = sem("head_probsT_hi")
        s_head = sem("head_summed")
        s_recip0 = sem("pair_recip")
        s_scaled = sem("pair_scaled")
        s_taken = sem("pair_taken")
        s_kept = sem("x0_kept")
        s_sd = sem("src_dst_ready")
        s_sdT = sem("src_dst_turned")
        s_sdT_hi = sem("src_dstT_hi")
        s_sdT_lo = sem("src_dstT_lo")
        s_z = sem("scores_ready")
        s_max = sem("max_ready")
        s_neg = sem("neg_max_ready")
        s_w = sem("exponents_ready")
        s_p = sem("probs_ready")
        s_pT = sem("probs_turned")
        s_pT_hi = sem("probsT_hi")
        s_pT_lo = sem("probsT_lo")
        s_xa_hi = sem("xa_hi")
        s_xa_lo = sem("xa_lo")
        s_agg = sem("agg_ready")
        s_recip = sem("recip_ready")
        s_nT = sem("nT_turned")
        s_nT_hi = sem("nT_hi")
        s_nT_lo = sem("nT_lo")
        s_up = sem("up_ready")
        s_g = sem("gelu_full")
        s_g_hi = sem("gelu_hi")
        s_g_lo = sem("gelu_lo")
        s_down = sem("down_tile_done")
        s_res_step = sem("residual_scaled")
        s_res = sem("residual_ready")
        s_aff_step = sem("x_scaled")
        s_aff = sem("x_ready")
        s_sum = {k: sem(f"{k}_sum") for k in NORMS}
        s_stat = {k: sem(f"{k}_stats") for k in NORMS}
        s_var = {k: sem(f"{k}_meanvar") for k in NORMS}
        s_eps = {k: sem(f"{k}_vareps") for k in NORMS}
        s_rstd = {k: sem(f"{k}_rstd") for k in NORMS}
        s_norm = {k: sem(f"{k}_norm") for k in NORMS}
        s_out = sem("out_stored")
        PER = {"l0": S, "n1": SLOTS, "n2": SLOTS, "end": S}

        block = ctx.enter_context(nc.Block())

        def f32(ap):
            return ap.bitcast(F32)

        def spread(ap, shape):
            return ap.broadcast_to(shape)

        def late_stream(t, n, ff, after):
            if n == 0 and ff:
                return t, S - 1
            if n == 3 and after:
                return t + 1, 0
            return None

        def wait_after_start(engine, semaphore, value):
            if not (isinstance(value, int) and value <= 0):
                engine.wait_ge(semaphore, value)

        def vector_waits(dve, semaphore, value):
            dve.wait_ge(semaphore, value)
            dve.memset(dve_mark[:, next(dve_marks)], 0.0)

        def pool_waits(pool, semaphore, value):
            pool.wait_ge(semaphore, value)
            pool.tensor_tensor(pool_mark[:, next(pool_marks)], half_neg[:, 0:1], half_neg[:, 0:1], ALU.mult)

        def all_partitions(ap, n):
            return ap.rearrange("(o n) -> o n", o=1).broadcast_to([P, n])

        def weight_blocks():
            for l in range(L):
                for part in range(KD):
                    yield True, l, part
                for part in range(2):
                    yield False, l, part

        blocks = list(weight_blocks())

        def stage_flat(b):
            return stage[b % 2]

        def weight_dst(b, t1, t2):
            up, l, part = blocks[b]
            if up:
                return t1[:, l, part, :]
            return t2[:, l, part * HF:(part + 1) * HF, :].rearrange("p f d -> p (f d)")

        @block.sync
        def _(sp):
            def load_x(it, d, s):
                g0 = it * (S * G) + (d * S + s) * G
                sp.dma_start(xin[:, s, :, :], x[bass.ds(g0, G), :, :].rearrange("g p d -> p g d"))\
                  .then_inc(s_x[s], 16)

            def load_adj(it, d, s):
                g0 = it * (S * G) + (d * S + s) * G
                sp.dma_start(adj_in[:, :, :], adj[bass.ds(g0, G), :, :].rearrange("g p d -> p g d"))\
                  .then_inc(s_adj, 16)

            def store(it, d, s):
                g0 = it * (S * G) + (d * S + s) * G
                sp.wait_ge(s_norm["end"], it * (S * G) + (d * S + s + 1) * G)
                sp.dma_start(out[bass.ds(g0, G), :, :].rearrange("g p d -> p g d"), final[:, :, :])\
                  .then_inc(s_out, 16)

            def load_next(it, d, s):
                if s == 0:
                    sp.wait_ge(s_edge0, it * S + (d + 1) * S)
                    load_adj(it, d + 1, 0)
                sp.wait_ge(s_kept, it * S + d * S + s + 1)
                load_x(it, d + 1, s)
                if s == 1:
                    sp.wait_ge(s_edge0, it * S + (d + 1) * S + 1)
                    load_adj(it, d + 1, 1)

            load_x(0, 0, 0)
            load_adj(0, 0, 0)
            load_x(0, 0, 1)
            for b, (up, l, part) in enumerate(blocks):
                if b >= 2:
                    sp.wait_ge(s_hi_done, b - 1)
                    sp.wait_ge(s_lo_done, b - 1)
                if up:
                    src = W1[l, part * P:(part + 1) * P, :]
                    dst = stage_flat(b)
                else:
                    src = W2[l].rearrange("(f p) d -> p f d", p=P)[:, part * HF:(part + 1) * HF, :]
                    dst = stage_flat(b).rearrange("p (f d) -> p f d", f=HF)
                sp.dma_start(dst, src).then_inc(s_stage[b % 2], 16)
                if b == 3:
                    sp.wait_ge(s_edge0, 1)
                    load_adj(0, 0, 1)
            for s in range(S):
                load_next(0, 0, s)
            with sp.Fori(0, TURNS - 2) as it:
                for s in range(S):
                    store(it, 0, s)
                    load_next(it, 1, s)
            for d in (TURNS - 2, TURNS - 1):
                for s in range(S):
                    store(0, d, s)
            sp.wait_ge(s_out, 16 * S * TURNS)

        @block.gpsimd
        def _(pool):
            pool.dma_start(rows_in[0:NB, :], b1.rearrange("l (f p) -> (l f) p", p=P)).then_inc(s_rows, 16)
            pool.dma_start(rows_in[NB:NB + NK, :], g1.rearrange("l (k p) -> (l k) p", p=P)).then_inc(s_rows, 16)
            pool.dma_start(rows_in[NB + NK:NB + 2 * NK, :], beta1.rearrange("l (k p) -> (l k) p", p=P))\
                .then_inc(s_rows, 16)
            pool.memset(ident[:, :], 0.0).then_inc(s_made, 1)
            pool.wait_ge(s_made, 1)
            pool.affine_select(out=ident[:, :], in_=ident[:, :], compare_op=ALU.not_equal, fill=1.0,
                               base=0, pattern=[[-1, P]], channel_multiplier=1).then_inc(s_made, 1)
            pool.memset(half_neg[:, :], -0.5).then_inc(s_made, 1)
            pool.memset(off_diag[:, :], 1.0).then_inc(s_made, 1)
            pool.memset(f32(sel[:, :]), 0.0).then_inc(s_made, 1)
            pool.memset(f32(rows0[:, :]), 0.0).then_inc(s_made, 1)
            pool.memset(f32(rows1[:, :]), 0.0).then_inc(s_made, 1)
            pool.memset(batt[:, :], 0.0).then_inc(s_made, 1)
            pool.wait_ge(s_made, 8)
            pool.affine_select(out=off_diag[:, :], in_=off_diag[:, :], compare_op=ALU.not_equal, fill=0.0,
                               base=0, pattern=[[-1, P]], channel_multiplier=1).then_inc(s_made, 1)
            pool.dma_start(batt[0:H, :], b_att.rearrange("(h o) -> h o", o=1)).then_inc(s_batt, 16)
            pool.wait_ge(s_ready, 1)
            pool.wait_ge(s_made, 9)

            def edges(t, s):
                wait_after_start(pool, s_h_w, t * (S * H) - (S - 1 - s) * H)
                pool_waits(pool, s_adj, t * (16 * S) + 16 * (s + 1))
                pool.tensor_scalar(edge0[:, s, :, :], adj_in[:, :, :], 0.0, MASKED, ALU.is_le, ALU.mult)\
                    .then_inc(s_edge0, 1)

            def self_edges(t, s):
                pool.wait_ge(s_edge0, t * S + s + 1)
                wait_after_start(pool, s_w, t * SLOTS - (S - 1 - s))
                pool.tensor_tensor(edge1[:, s, :, :], edge0[:, s, :, :],
                                   spread(off_diag[:, :].rearrange("p (o n) -> p o n", o=1), [P, G, N]),
                                   ALU.mult).then_inc(s_edge1, 1)

            def inverse_root(t, kind, n):
                pool.wait_ge(s_eps[kind], t * PER[kind] + n + 1)
                pool.tensor_tensor(rstd[kind][:, :], vareps[kind][:, :], half_neg[:, :], ALU.pow)\
                    .then_inc(s_rstd[kind], 1)

            def residual(t, n, g):
                l, s = n // S, n % S
                pool.wait_ge(s_nT, t * (SLOTS * KD) + (n + 1) * KD)
                pool.tensor_tensor(xs[:, s, g, :], xs[:, s, g, :], gamma1[:, l, :], ALU.mult)\
                    .then_inc(s_res_step, 1)
                pool.wait_ge(s_res_step, t * (SLOTS * G) + n * G + g + 1)
                pool.tensor_tensor(xs[:, s, g, :], xs[:, s, g, :], shift1[:, l, :], ALU.add).then_inc(s_res, 1)

            def affine(t, n, g):
                l, s = n // S, n % S
                if n + S < SLOTS:
                    pool.wait_ge(s_sd, t * (SLOTS * G) + (n + S) * G + g + 1)
                else:
                    pool.wait_ge(s_norm["n2"], t * (SLOTS * G) + n * G + g + 1)
                pool.tensor_tensor(xs[:, s, g, :], xs[:, s, g, :], gamma2[:, l, :], ALU.mult)\
                    .then_inc(s_aff_step, 1)
                pool.wait_ge(s_aff_step, t * (SLOTS * G) + n * G + g + 1)
                pool.tensor_tensor(xs[:, s, g, :], xs[:, s, g, :], shift2[:, l, :], ALU.add)\
                    .then_inc(s_aff, 1)

            def slot(t, n, ff=True, before=True, after=True):
                pt, pn = (t, n - 1) if n else (t - 1, SLOTS - 1)
                if ff:
                    residual(t, n, 0)
                    if before:
                        inverse_root(pt, "n2", pn)
                    if n == 0:
                        inverse_root(t, "l0", 1)
                    if n == 3 and after:
                        inverse_root(t + 1, "l0", 0)
                    for g in range(1, G):
                        residual(t, n, g)
                    if before:
                        for g in range(G):
                            affine(pt, pn, g)
                elif n == 3:
                    inverse_root(t + 1, "l0", 0)
                if after and n % 3 == 0:
                    edges(t + 1, n // 3)
                if after and n in (4, 5):
                    self_edges(t + 1, n - 4)
                if ff and before and pn >= SLOTS - S:
                    inverse_root(pt, "end", pn - (SLOTS - S))
                if (ff and n + 1 < SLOTS) or (n + 1 == SLOTS and after):
                    mt, m = (t, n + 1) if n + 1 < SLOTS else (t + 1, 0)
                    inverse_root(mt, "n1", m)

            for n in range(SLOTS):
                slot(-1, n, ff=False, before=False)
            slot(0, 0, before=False)
            with pool.Fori(0, TURNS - 2) as it:
                for n in range(1, SLOTS):
                    slot(it, n)
                slot(it + 1, 0)
            for n in range(1, SLOTS):
                slot(TURNS - 2, n)
            for n in range(SLOTS):
                slot(TURNS - 1, n, after=False)
            inverse_root(TURNS - 1, "n2", SLOTS - 1)
            for g in range(G):
                affine(TURNS - 1, SLOTS - 1, g)
            inverse_root(TURNS - 1, "end", S - 1)

        @block.scalar
        def _(act):
            act.dma_start(wp_in, w_proj.rearrange("(k p) d -> p k d", p=P)).then_inc(s_wp, 16)
            act.dma_start(watt_b, all_partitions(w_att.rearrange("h k -> (h k)"), H * K2)
                          .rearrange("p (h k) -> p h k", h=H)).then_inc(s_wp, 16)
            for dst, src, n in ((attw, attn_w, L * 2 * D), (gamma1, g1, L * D), (shift1, beta1, L * D),
                                (gamma2, g2, L * D), (shift2, beta2, L * D)):
                act.dma_start(dst[:, :, :].rearrange("p l d -> p (l d)"),
                              all_partitions(src.rearrange("l d -> (l d)"), n)).then_inc(s_consts, 16)
            act.dma_start(attb[:, :], all_partitions(attn_b, L)).then_inc(s_consts, 16)
            act.wait_ge(s_prep, 4 * KD)
            act.dma_start(b2_b.rearrange("p l d -> p (l d)"), all_partitions(b2.rearrange("l d -> (l d)"), L * D))\
               .then_inc(s_consts, 16)
            def weights_hi(b):
                up, l, part = blocks[b]
                act.wait_ge(s_stage[b % 2], 16 * (b // 2 + 1))
                if up:
                    act.wait_ge(s_cols, 1)
                    c = NB + l * KD + part
                    act.activation(weight_dst(b, w1_hi, w2_hi), stage_flat(b), ACT.Identity,
                                   scale=cols[:, c:c + 1]).then_inc(s_hi_done, 1)
                else:
                    act.activation(weight_dst(b, w1_hi, w2_hi), stage_flat(b), ACT.Copy)\
                       .then_inc(s_hi_done, 1)

            def xT_hi(t, s, g):
                act.wait_ge(s_hb, t * (S * USES) + s * USES + use_index["x", g] + 1)
                h = slice((g % 2) * KD * P, (g % 2 + 1) * KD * P)
                act.activation(hT_hi[:, h], HB[:, 0:KD * P], ACT.Copy).then_inc(s_xT_hi, 1)

            def xh_parts(t, s, g):
                act.wait_ge(s_proj, t * (S * G) + s * G + g + 1)
                act.activation(rows0[0:2 * H, g * P:(g + 1) * P], HO[0:2 * H, D:D + P], ACT.Identity,
                               bias=batt[:, :])
                act.activation(xh_hi[:, g, :], HO[:, 0:D], ACT.Copy).then_inc(s_xh_hi, 1)

            def head_exp(t, s, h):
                act.wait_ge(s_h_w, t * (S * H) + s * H + h + 1)
                for g in range(G):
                    c = slice(g * P, (g + 1) * P)
                    ins = act.activation(w0[:, h % 4, c], w0[:, h % 4, c], ACT.Exp, bias=top0[:, h % 4, g:g + 1],
                                         accum_out=sums0[:, h // 2, g, h % 2:h % 2 + 1])
                ins.then_inc(s_h_p, 1)

            def head_probsT_hi(t, s, h):
                act.wait_ge(s_hb, t * (S * USES) + s * USES + use_index["probs", h] + 1)
                act.activation(hT_hi[:, :], HB[:, :], ACT.Copy).then_inc(s_hT_hi, 1)

            def keep(t, s):
                act.wait_ge(s_xa_lo, t * SLOTS + s + 1)
                wait_after_start(act, s_sum["end"], t * (S * G) - (S - 1 - s) * G)
                act.activation(x0[:, s, :, :], xin[:, s, :, :], ACT.Copy).then_inc(s_kept, 1)

            def sdT_hi(t, m):
                act.wait_ge(s_sdT, t * SLOTS + m + 1)
                act.activation(rows1[0:2 * G, :], T[0:2 * G, 0:P], ACT.Copy).then_inc(s_sdT_hi, 1)

            def exponential(t, m):
                act.wait_ge(s_w, t * SLOTS + m + 1)
                for g in range(G):
                    c = slice(g * P, (g + 1) * P)
                    ins = act.activation(w1[:, c], w1[:, c], ACT.Exp, bias=top1[:, g:g + 1],
                                         accum_out=sums1[:, g:g + 1])
                ins.then_inc(s_p, 1)

            def probsT_hi(t, m):
                act.wait_ge(s_pT, t * SLOTS + m + 1)
                act.activation(nT_hi[:, 0, :], T[:, :], ACT.Copy).then_inc(s_pT_hi, 1)

            def nT_hi_parts(t, m):
                for k in range(KD):
                    act.wait_ge(s_nT, t * (SLOTS * KD) + m * KD + k + 1)
                    act.activation(nT_hi[:, k, :], [Z, T][k][:, :], ACT.Copy).then_inc(s_nT_hi, 1)

            def heads_step(t, s, step):
                for g in range(G):
                    if step == X_AT[g] + 1:
                        xT_hi(t, s, g)
                    if step == X_AT[g] + 2:
                        xh_parts(t, s, g)
                for h in range(H):
                    if step == TURN_AT[h] + 1:
                        head_probsT_hi(t, s, h)

            def slot(t, n, ff=True, after=True):
                has_m = (ff and n + 1 < SLOTS) or (n + 1 == SLOTS and after)
                mt, m = (t, n + 1) if n + 1 < SLOTS else (t + 1, 0)
                late, sd_at = late_stream(t, n, ff, after), SD_AT + (n == 0)
                for f in range(FT):
                    if ff:
                        e = n * FT + f
                        act.wait_ge(s_up, t * (SLOTS * FT) + e + 1)
                        b = bias1[:, (n // S) * FT + f:(n // S) * FT + f + 1]
                        wait_after_start(act, s_g_lo, t * (SLOTS * FT) + e - 1)
                        act.activation(g_full[:, f % 2, :], up_bank[f % 2][:, :], ACT.Gelu, bias=b)\
                           .then_inc(s_g, 1)
                        if f < HI_BY_ACT:
                            wait_after_start(act, s_down, t * (SLOTS * FT) + e - R + 1)
                            act.activation(G_hi[:, e % R, :], up_bank[f % 2][:, :], ACT.Gelu, bias=b)\
                               .then_inc(s_g_hi, 1)
                    if not ff and f in WEIGHTS_AT:
                        weights_hi(2 * n + WEIGHTS_AT.index(f))
                    if has_m and f == sd_at + 1:
                        sdT_hi(mt, m)
                    if has_m and f == PROBS_AT:
                        exponential(mt, m)
                    batch = [h for h in range(H) if EXP_AT[h] == n % 3 * FT + f and after]
                    for h in batch[:1]:
                        head_exp(t + 1, n // 3, h)
                    if has_m and f == PROBS_AT:
                        probsT_hi(mt, m)
                    for h in batch[1:]:
                        head_exp(t + 1, n // 3, h)
                    if f < LATE and late:
                        heads_step(*late, SPAN + f)
                    if after:
                        heads_step(t + 1, n // 3, n % 3 * FT + f)
                    if f == KEEP_AT and n == 0 and ff:
                        keep(t, 1)
                    if f == KEEP_AT and n + 1 == SLOTS and after:
                        keep(t + 1, 0)
                if has_m:
                    nT_hi_parts(mt, m)

            for n in range(SLOTS):
                slot(-1, n, ff=False)
            act.wait_ge(s_bias, 1)
            slot(0, 0)
            with act.Fori(0, TURNS - 2) as it:
                for n in range(1, SLOTS):
                    slot(it, n)
                slot(it + 1, 0)
            for n in range(1, SLOTS):
                slot(TURNS - 2, n)
            for n in range(SLOTS):
                slot(TURNS - 1, n, after=False)

        @block.tensor
        def _(pe):
            def split_matmul(dst, a_hi, a_lo, b_hi, b_lo, first, last):
                pe.matmul(dst, a_hi, b_hi, start=first, stop=False)
                pe.matmul(dst, a_hi, b_lo, start=False, stop=False)
                return pe.matmul(dst, a_lo, b_hi, start=False, stop=last)

            pe.wait_ge(s_made, 2)
            pe.wait_ge(s_rows, 48)
            nr = NB + 2 * NK
            pe.transpose(T[:, 0:nr], rows_in, ident[0:nr, 0:nr]).then_inc(s_cols_ps, 1)
            pe.wait_ge(s_cols, 1)
            pe.wait_ge(s_ready, 1)

            def heads_bank_free(t, s, use):
                wait_after_start(pe, s_hb_read, t * (S * USES) + s * USES + use_index[use])

            def weights_bias(b):
                up, l, part = blocks[b]
                if not up:
                    return
                pe.wait_ge(s_stage[b % 2], 16 * (b // 2 + 1))
                c = NB + NK + l * KD + part
                for f in range(FT):
                    mm = pe.matmul([U0, U1][part][:, l * FT + f:l * FT + f + 1],
                                   stage_flat(b)[:, f * P:(f + 1) * P], cols[:, c:c + 1], start=True, stop=True)
                mm.then_inc(s_bmm, 1)

            def turn_x(t, s, g):
                if g == 0:
                    pe.wait_ge(s_x[s], t * 16 + 16)
                heads_bank_free(t, s, ("x", g))
                for k in range(KD):
                    ins = pe.transpose(HB[:, k * P:(k + 1) * P], xin[:, s, g, k * P:(k + 1) * P], ident[:, :])
                ins.then_inc(s_hb, 1)

            def project(t, s, g):
                pe.wait_ge(s_hb_read, t * (S * USES) + s * USES + use_index["x", g] + 1)
                if g == 0:
                    wait_after_start(pe, s_taken, (t * S + s) * (H // 2))
                else:
                    pe.wait_ge(s_xh_lo, t * (S * G) + s * G + g)
                c = [slice(((g % 2) * KD + k) * P, ((g % 2) * KD + k + 1) * P) for k in range(KD)]
                for k in range(KD):
                    split_matmul(HO[:, 0:D], hT_hi[:, c[k]], hT_lo[:, c[k]], wp_hi[:, k, 0:D], wp_lo[:, k, 0:D],
                                 k == 0, k == KD - 1)
                for k in range(KD):
                    mm = split_matmul(HO[0:2 * H, D:D + P], wp_hi[:, k, D:PW], wp_lo[:, k, D:PW],
                                      hT_hi[:, c[k]], hT_lo[:, c[k]], k == 0, k == KD - 1)
                mm.then_inc(s_proj, 1)

            def head_scores(t, s, h, attention_done):
                if h == 0:
                    pe.wait_ge(s_xh_lo, t * (S * G) + (s + 1) * G)
                wait_after_start(pe, s_h_max, t * (S * H) + s * H + h)
                if attention_done is not None:
                    pe.wait_ge(s_max, attention_done)
                K = 32 + 2 * H
                pe.matmul(Z[:, :], spread(sel[:, H + h:H + h + 1], [K, P]), rows0[:, :], start=True, stop=False)
                for g in range(G):
                    c = slice(g * P, (g + 1) * P)
                    mm = pe.matmul(Z[:, c], rows0[:, c], spread(sel[:, h:h + 1], [K, P]),
                                   start=False, stop=g == G - 1)
                mm.then_inc(s_h_z, 1)

            def turn_head(t, s, h):
                heads_bank_free(t, s, ("probs", h))
                pe.wait_ge(s_h_p, t * (S * H) + s * H + h + 1)
                for g in range(G):
                    c = slice(g * P, (g + 1) * P)
                    ins = pe.transpose(HB[:, c], w0[:, h % 4, c], ident[:, :])
                ins.then_inc(s_hb, 1)

            def head_sum(t, s, h):
                pe.wait_ge(s_hb_read, t * (S * USES) + s * USES + use_index["probs", h] + 1)
                pair = h // 2
                if pair and h % 2 == 0:
                    pe.wait_ge(s_taken, (t * S + s) * (H // 2) + pair)
                for g in range(G):
                    c = slice(g * P, (g + 1) * P)
                    o = (pair % 2) * D + g * (2 * KH) + (h % 2) * KH
                    mm = split_matmul(HO[:, o:o + KH], hT_hi[:, c], hT_lo[:, c],
                                      xh_hi[:, g, h * KH:(h + 1) * KH], xh_lo[:, g, h * KH:(h + 1) * KH],
                                      True, True)
                mm.then_inc(s_head, 1)

            def heads_step(t, s, step, attention_done=None):
                for g in range(G):
                    if step == X_AT[g] + 1:
                        project(t, s, g)
                for h in range(H):
                    if step == TURN_AT[h] + 1:
                        head_sum(t, s, h)
                for h in range(H):
                    if step == TURN_AT[h]:
                        turn_head(t, s, h)
                for g in range(G):
                    if step == X_AT[g]:
                        turn_x(t, s, g)
                for h in range(H):
                    if step == SCORE_AT[h]:
                        head_scores(t, s, h, attention_done)

            def turn_sd(t, m):
                pe.wait_ge(s_sd, t * (SLOTS * G) + (m + 1) * G)
                pe.transpose(T[0:2 * G, 0:P], sd[:, :], ident[:, :]).then_inc(s_sdT, 1)

            def scores(t, m, heads_scored):
                pe.wait_ge(s_sdT_lo, t * SLOTS + m + 1)
                if heads_scored is not None:
                    pe.wait_ge(s_h_max, heads_scored)
                K = 32 + 2 * G
                for g in range(G):
                    c = slice(g * P, (g + 1) * P)
                    pe.matmul(Z[:, c], spread(sel[0:K, G + g:G + g + 1], [K, P]), rows1[:, :], start=True, stop=False)
                    mm = pe.matmul(Z[:, c], rows1[:, :], spread(sel[0:K, g:g + 1], [K, P]), start=False, stop=True)
                mm.then_inc(s_z, 1)

            def turn_probs(t, m):
                pe.wait_ge(s_p, t * SLOTS + m + 1)
                for g in range(G):
                    c = slice(g * P, (g + 1) * P)
                    ins = pe.transpose(T[:, c], w1[:, c], ident[:, :])
                ins.then_inc(s_pT, 1)

            def aggregate(t, m, graphs):
                pe.wait_ge(s_xa_lo, t * SLOTS + m + 1)
                pe.wait_ge(s_pT_lo, t * SLOTS + m + 1)
                for g in graphs:
                    c = slice(g * P, (g + 1) * P)
                    split_matmul(half(agg_bank[g], g), nT_hi[:, 0, c], nT_lo[:, 0, c],
                                 xa_hi[:, g, :], xa_lo[:, g, :], True, True).then_inc(s_agg, 1)

            def keep_busy(t, n):
                pe.wait_ge(s_g_hi, t * (SLOTS * FT) + (n + 1) * FT - 1)
                for _ in range(FILL):
                    pe.matmul(U0[:, :], w1_hi[:, 0, 0, 0:P], w1_hi[:, 0, 0, 0:NG], start=True, stop=True)

            def turn_norm(t, m):
                for k in range(KD):
                    for g in range(G):
                        if k == 0:
                            pe.wait_ge(s_norm["n1"], t * (SLOTS * G) + m * G + g + 1)
                        ins = pe.transpose([Z, T][k][:, g * P:(g + 1) * P],
                                           xs[:, m % S, g, k * P:(k + 1) * P], ident[:, :])
                    ins.then_inc(s_nT, 1)

            def up(t, n, f):
                l = n // S
                e = n * FT + f
                c = slice(f * P, (f + 1) * P)
                if f == 0:
                    pe.wait_ge(s_nT_lo, t * (SLOTS * KD) + n * KD + 1)
                wait_after_start(pe, s_g_hi, t * (SLOTS * FT) + e - 1)
                for k in range(KD):
                    if f == 0 and k == KD - 1:
                        pe.wait_ge(s_nT_lo, t * (SLOTS * KD) + (n + 1) * KD)
                    mm = split_matmul(up_bank[f % 2][:, :], w1_hi[:, l, k, c], w1_lo[:, l, k, c],
                                      nT_hi[:, k, :], nT_lo[:, k, :], k == 0, k == KD - 1)
                mm.then_inc(s_up, 1)

            def down(t, n, f):
                l = n // S
                e = n * FT + f
                if f == 0:
                    wait_after_start(pe, s_sum["n2"], t * (SLOTS * G) + n * G)
                pe.wait_ge(s_g_lo, t * (SLOTS * FT) + e + 1)
                for g in range(G):
                    c = slice(g * P, (g + 1) * P)
                    mm = split_matmul(half(down_bank[g], g), G_hi[:, e % R, c], G_lo[:, e % R, c],
                                      w2_hi[:, l, f, :], w2_lo[:, l, f, :], f == 0 and g % 2 == 0, f == FT - 1 and g % 2 == 1)
                mm.then_inc(s_down, 1)

            def slot(t, n, ff=True, after=True):
                has_m = (ff and n + 1 < SLOTS) or (n + 1 == SLOTS and after)
                mt, m = (t, n + 1) if n + 1 < SLOTS else (t + 1, 0)
                late, sd_at = late_stream(t, n, ff, after), SD_AT + (n == 0)
                if ff:
                    up(t, n, 0)
                    up(t, n, 1)
                for f in range(FT):
                    if ff:
                        if f + 2 < FT:
                            up(t, n, f + 2)
                    elif f in WEIGHTS_AT:
                        weights_bias(2 * n + WEIGHTS_AT.index(f))
                    if has_m:
                        if f == sd_at:
                            turn_sd(mt, m)
                        if f == sd_at + 1:
                            done = sum(at < n % 3 * FT + f for at in SCORE_AT)
                            scores(mt, m, (t + 1) * (S * H) + n // 3 * H + done if after and done else None)
                        if f == PROBS_AT:
                            turn_probs(mt, m)
                        if f == SUM_AT:
                            done = sum(at < n % 3 * FT + f for at in SCORE_AT)
                            if after and done:
                                pe.wait_ge(s_h_max, (t + 1) * (S * H) + n // 3 * H + done)
                            aggregate(mt, m, range(0, 2))
                        if f == SUM2_AT:
                            aggregate(mt, m, range(2, G))
                    if ff:
                        down(t, n, f)
                    if f < LATE and late:
                        heads_step(*late, SPAN + f)
                    if after:
                        heads_step(t + 1, n // 3, n % 3 * FT + f,
                                   mt * SLOTS + m + 1 if has_m and f > sd_at else None)
                if has_m:
                    if ff:
                        keep_busy(t, n)
                    turn_norm(mt, m)

            for n in range(SLOTS):
                slot(-1, n, ff=False)
            pe.wait_ge(s_bias, 1)
            slot(0, 0)
            with pe.Fori(0, TURNS - 2) as it:
                for n in range(1, SLOTS):
                    slot(it, n)
                slot(it + 1, 0)
            for n in range(1, SLOTS):
                slot(TURNS - 2, n)
            for n in range(SLOTS):
                slot(TURNS - 1, n, after=False)

        @block.vector
        def _(dve):
            steps = [0]

            def prep(ins):
                steps[0] += 1
                ins.then_inc(s_prep, 1)
                dve.wait_ge(s_prep, steps[0])

            dve.wait_ge(s_wp, 32)
            for k in range(KD):
                for side in range(2):
                    prep(dve.tensor_tensor(prod.rearrange("p (h c) -> p h c", h=H),
                                           wp_in[:, k, :].rearrange("p (h c) -> p h c", h=H),
                                           watt_b[:, :, side * KH:(side + 1) * KH], ALU.mult))
                    prep(dve.tensor_reduce(wsum[:, k, side * H:(side + 1) * H],
                                           prod.rearrange("p (h c) -> p h c", h=H), AX_X, ALU.add))
            for part, src in ((slice(0, D), wp_in), (slice(D, PW), wsum)):
                prep(dve.tensor_copy(wp_hi[:, :, part], src))
                prep(dve.tensor_tensor(wp_lo[:, :, part], src, f32(wp_hi[:, :, part]), ALU.subtract))
            dve.wait_ge(s_cols_ps, 1)
            dve.tensor_copy(cols[:, :], T[:, 0:NB + 2 * NK]).then_inc(s_cols, 1)
            dve.wait_ge(s_made, 9)
            for first in (0, 32):
                some = slice(first, first + 2 * H)
                prep(dve.tensor_copy(sel[some, :], ident[some, some]))
            dve.wait_ge(s_cols, 1)
            dve.wait_ge(s_consts, 16 * 7)
            dve.wait_ge(s_batt, 16)
            dve.wait_ge(s_made, 9)
            prep(dve.tensor_tensor(shift1[:, :, :], shift1[:, :, :], b2_b, ALU.add))
            for l in range(1, L):
                for side in range(2):
                    prep(dve.tensor_tensor_reduce(
                        out=prod, in0=attw[:, l, side * D:(side + 1) * D], in1=shift2[:, l - 1, :], scale=1.0,
                        scalar=attb[:, l:l + 1], op0=ALU.mult, op1=ALU.add, accum_out=recip1[:, 0:1]))
                    prep(dve.tensor_copy(attb[:, l:l + 1], recip1[:, 0:1]))
                    prep(dve.tensor_tensor(attw[:, l, side * D:(side + 1) * D],
                                           attw[:, l, side * D:(side + 1) * D], gamma2[:, l - 1, :], ALU.mult))
            dve.tensor_copy(recip1[:, 3:4], attb[:, 0:1]).then_inc(s_ready, 1)

            def low_part(dst, src, hi):
                return dve.tensor_tensor(dst, src, f32(hi), ALU.subtract)

            def weights_lo(b):
                is_up, l, part = blocks[b]
                dve.wait_ge(s_hi_done, b + 1)
                hi, lo = weight_dst(b, w1_hi, w2_hi), weight_dst(b, w1_lo, w2_lo)
                if is_up:
                    dve.wait_ge(s_bmm, sum(up for up, _, _ in blocks[:b + 1]))
                    c = NB + l * KD + part
                    dve.scalar_tensor_tensor(lo, stage_flat(b), cols[:, c:c + 1], f32(hi),
                                             ALU.mult, ALU.subtract).then_inc(s_lo_done, 1)
                else:
                    dve.tensor_tensor(lo, stage_flat(b), f32(hi), ALU.subtract).then_inc(s_lo_done, 1)

            def xT_lo(t, s, g):
                dve.wait_ge(s_xT_hi, t * (S * G) + s * G + g + 1)
                h = slice((g % 2) * KD * P, (g % 2 + 1) * KD * P)
                low_part(hT_lo[:, h], HB[:, 0:KD * P], hT_hi[:, h]).then_inc(s_hb_read, 1)

            def xh_parts(t, s, g):
                dve.wait_ge(s_xh_hi, t * (S * G) + s * G + g + 1)
                c = slice(g * P, (g + 1) * P)
                dve.scalar_tensor_tensor(rows0[32:32 + 2 * H, c], HO[0:2 * H, D:D + P], batt[:, :],
                                         f32(rows0[0:2 * H, c]), ALU.add, ALU.subtract)
                low_part(xh_lo[:, g, :], HO[:, 0:D], xh_hi[:, g, :]).then_inc(s_xh_lo, 1)

            def head_exponents(t, s, h):
                count = t * (S * H) + s * H + h + 1
                if h == 0:
                    vector_waits(dve, s_edge0, t * S + s + 1)
                vector_waits(dve, s_h_z, count)
                w = w0[:, h % 4, :]
                for g in range(G):
                    c = slice(g * P, (g + 1) * P)
                    ins = dve.tensor_tensor_reduce(out=w[:, c], in0=Z[:, c], in1=edge0[:, s, g, :], scale=1.0,
                                                   scalar=-3.0e38, op0=ALU.add, op1=ALU.max,
                                                   accum_out=row_max0[:, g:g + 1])
                ins.then_inc(s_h_max, 1)
                dve.wait_ge(s_h_max, count)
                dve.tensor_scalar(neg_max0[:, :], row_max0[:, :], -1.0, None, ALU.mult).then_inc(s_h_neg, 1)
                dve.wait_ge(s_h_neg, count)
                dve.scalar_tensor_tensor(top0[:, h % 4, :], neg_max0[:, :], SLOPE, neg_max0[:, :],
                                         ALU.mult, ALU.min)
                dve.scalar_tensor_tensor(w, w, SLOPE, w, ALU.mult, ALU.max).then_inc(s_h_w, 1)

            def head_probsT_lo(t, s, h):
                dve.wait_ge(s_hT_hi, t * (S * H) + s * H + h + 1)
                low_part(hT_lo[:, :], HB[:, :], hT_hi[:, :]).then_inc(s_hb_read, 1)

            def take_pair(t, s, pair):
                count = (t * S + s) * (H // 2) + pair + 1
                dve.wait_ge(s_head, t * (S * H) + s * H + 2 * pair + 2)
                dve.reciprocal(recip0[:, :, :], sums0[:, pair, :, :]).then_inc(s_recip0, 1)
                dve.wait_ge(s_recip0, count)
                o = (pair % 2) * D
                sums = HO[:, o:o + D]
                dve.tensor_tensor(sums.rearrange("p (x c) -> p x c", c=KH), sums.rearrange("p (x c) -> p x c", c=KH),
                                  spread(recip0[:, :, :].rearrange("p g (i o) -> p (g i) o", o=1), [P, 2 * G, KH]),
                                  ALU.mult).then_inc(s_scaled, 1)
                dve.wait_ge(s_scaled, count)
                c = slice(2 * pair * KH, 2 * (pair + 1) * KH)
                dve.scalar_tensor_tensor(xin[:, s, :, c], sums.rearrange("p (g c) -> p g c", g=G), 0.0,
                                         xin[:, s, :, c], ALU.max, ALU.add).then_inc(s_taken, 1)

            def row_stats(t, kind, n, g, rows, done, count):
                dve.wait_ge(done, count)
                dve.bn_stats(stats[kind][:, g, :], rows).then_inc(s_stat[kind], 1)

            def mean_var(t, kind, n):
                for g in range(G):
                    if g == 0:
                        vector_waits(dve, s_stat[kind], t * (PER[kind] * G) + (n + 1) * G)
                    ins = dve.bn_aggr(meanvar[kind][:, g, :], stats[kind][:, g, :])
                ins.then_inc(s_var[kind], 1)
                dve.wait_ge(s_var[kind], t * PER[kind] + n + 1)
                dve.tensor_scalar(vareps[kind][:, :], meanvar[kind][:, :, 1], EPS, None, ALU.add)\
                   .then_inc(s_eps[kind], 1)

            def normalize(t, kind, n, g, rows):
                if g == 0:
                    dve.wait_ge(s_rstd[kind], t * PER[kind] + n + 1)
                dve.tensor_scalar(rows, rows, meanvar[kind][:, g, 0:1], rstd[kind][:, g:g + 1],
                                  ALU.subtract, ALU.mult).then_inc(s_norm[kind], 1)

            def heads_stats(t, s):
                for g in range(G):
                    row_stats(t, "l0", s, g, xin[:, s, g, :], s_taken, (t * S + s + 1) * (H // 2))
                mean_var(t, "l0", s)

            def heads_norm(t, s):
                for g in range(G):
                    normalize(t, "l0", s, g, xin[:, s, g, :])

            def heads_step(t, s, step):
                for pair in range(H // 2):
                    if step == TAKE_AT[pair]:
                        take_pair(t, s, pair)
                for g in range(G):
                    if step == X_AT[g] + 2:
                        xh_parts(t, s, g)
                for h in range(H):
                    if step == TURN_AT[h] + 1:
                        head_probsT_lo(t, s, h)
                for g in range(G):
                    if step == X_AT[g] + 1:
                        xT_lo(t, s, g)
                for h in range(H):
                    if step == SCORE_AT[h] + 1:
                        head_exponents(t, s, h)

            def gelu_parts(t, n, f):
                e = n * FT + f
                count = t * (SLOTS * FT) + e + 1
                if f >= HI_BY_ACT:
                    dve.wait_ge(s_g, count)
                    wait_after_start(dve, s_down, count - R)
                    dve.tensor_copy(G_hi[:, e % R, :], g_full[:, f % 2, :]).then_inc(s_g_hi, 1)
                dve.wait_ge(s_g_hi, count)
                low_part(G_lo[:, e % R, :], g_full[:, f % 2, :], G_hi[:, e % R, :]).then_inc(s_g_lo, 1)

            def src_dst(t, m, g):
                l, s = m // S, m % S
                rows = (xin if l == 0 else xs)[:, s, g, :]
                if l == 0:
                    dve.wait_ge(s_norm["l0"], t * (S * G) + s * G + g + 1)
                else:
                    dve.wait_ge(s_norm["n2"], t * (SLOTS * G) + (m - S) * G + g + 1)
                if g:
                    dve.wait_ge(s_sd, t * (SLOTS * G) + m * G + g)
                dve.tensor_tensor_reduce(out=w1[:, 0:D], in0=rows, in1=attw[:, l, 0:D], scale=1.0,
                                         scalar=attb[:, l:l + 1], op0=ALU.mult, op1=ALU.add,
                                         accum_out=sd[:, g:g + 1])
                dve.tensor_tensor_reduce(out=w1[:, D:2 * D], in0=rows, in1=attw[:, l, D:2 * D], scale=1.0,
                                         scalar=0.0, op0=ALU.mult, op1=ALU.add,
                                         accum_out=sd[:, G + g:G + g + 1]).then_inc(s_sd, 1)

            def sdT_lo(t, m):
                dve.wait_ge(s_sdT_hi, t * SLOTS + m + 1)
                low_part(rows1[32:32 + 2 * G, :], T[0:2 * G, 0:P], rows1[0:2 * G, :]).then_inc(s_sdT_lo, 1)

            def xa_parts(t, m):
                l, s = m // S, m % S
                src = (xin if l == 0 else xs)[:, s, :, :]
                if l == 0:
                    dve.wait_ge(s_norm["l0"], t * (S * G) + (s + 1) * G)
                else:
                    dve.wait_ge(s_aff, t * (SLOTS * G) + (m - S + 1) * G)
                wait_after_start(dve, s_agg, t * (SLOTS * G) + m * G)
                dve.tensor_copy(xa_hi[:, :, :], src).then_inc(s_xa_hi, 1)
                dve.wait_ge(s_xa_hi, t * SLOTS + m + 1)
                low_part(xa_lo[:, :, :], src, xa_hi[:, :, :]).then_inc(s_xa_lo, 1)

            def exponents(t, m):
                count = t * SLOTS + m + 1
                if m < S:
                    vector_waits(dve, s_edge1, t * S + m + 1)
                vector_waits(dve, s_z, count)
                for g in range(G):
                    c = slice(g * P, (g + 1) * P)
                    ins = dve.tensor_tensor_reduce(out=w1[:, c], in0=Z[:, c], in1=edge1[:, m % S, g, :], scale=1.0,
                                                   scalar=-3.0e38, op0=ALU.add, op1=ALU.max,
                                                   accum_out=row_max1[:, g:g + 1])
                ins.then_inc(s_max, 1)
                dve.wait_ge(s_max, count)
                dve.tensor_scalar(neg_max1[:, :], row_max1[:, :], -1.0, None, ALU.mult).then_inc(s_neg, 1)
                dve.wait_ge(s_neg, count)
                dve.scalar_tensor_tensor(top1[:, :], neg_max1[:, :], SLOPE, neg_max1[:, :], ALU.mult, ALU.min)
                dve.scalar_tensor_tensor(w1[:, :], w1[:, :], SLOPE, w1[:, :], ALU.mult, ALU.max).then_inc(s_w, 1)

            def probsT_lo(t, m):
                dve.wait_ge(s_pT_hi, t * SLOTS + m + 1)
                low_part(nT_lo[:, 0, :], T[:, :], nT_hi[:, 0, :]).then_inc(s_pT_lo, 1)

            def attention_sums(t, m, graphs):
                l, s = m // S, m % S
                if 0 in graphs:
                    if l == 0:
                        dve.wait_ge(s_kept, t * S + m + 1)
                    dve.wait_ge(s_p, t * SLOTS + m + 1)
                    dve.reciprocal(recip1[:, :], sums1[:, :]).then_inc(s_recip, 1)
                    dve.wait_ge(s_recip, t * SLOTS + m + 1)
                dve.wait_ge(s_agg, t * (SLOTS * G) + m * G + graphs[-1] + 1)
                for g in graphs:
                    dve.scalar_tensor_tensor(xs[:, s, g, :], half(agg_bank[g], g), recip1[:, g:g + 1],
                                             (x0 if l == 0 else xs)[:, s, g, :], ALU.mult, ALU.add)\
                       .then_inc(s_sum["n1"], 1)
                for g in graphs:
                    row_stats(t, "n1", m, g, xs[:, s, g, :], s_sum["n1"], t * (SLOTS * G) + m * G + g + 1)

            def attention_norm(t, m):
                for g in range(G):
                    normalize(t, "n1", m, g, xs[:, m % S, g, :])

            def nT_lo_parts(t, m):
                for k in range(KD):
                    dve.wait_ge(s_nT_hi, t * (SLOTS * KD) + m * KD + k + 1)
                    low_part(nT_lo[:, k, :], [Z, T][k][:, :], nT_hi[:, k, :]).then_inc(s_nT_lo, 1)

            def feed_forward_sum(t, n, g):
                s = n % S
                dve.wait_ge(s_down, t * (SLOTS * FT) + (n + 1) * FT)
                dve.wait_ge(s_res, t * (SLOTS * G) + n * G + g + 1)
                dve.tensor_tensor(xs[:, s, g, :], half(down_bank[g], g), xs[:, s, g, :], ALU.add)\
                   .then_inc(s_sum["n2"], 1)

            def feed_forward_stats(t, n):
                for g in range(G):
                    row_stats(t, "n2", n, g, xs[:, n % S, g, :], s_sum["n2"], t * (SLOTS * G) + n * G + g + 1)
                mean_var(t, "n2", n)

            def feed_forward_norm(t, n):
                for g in range(G):
                    normalize(t, "n2", n, g, xs[:, n % S, g, :])

            def end_sum(t, s, g):
                if g == 0:
                    wait_after_start(dve, s_out, t * (16 * S) + 16 * s)
                dve.wait_ge(s_aff, t * (SLOTS * G) + (SLOTS - S + s) * G + g + 1)
                dve.tensor_tensor(final[:, g, :], xs[:, s, g, :], x0[:, s, g, :], ALU.add)\
                   .then_inc(s_sum["end"], 1)
                row_stats(t, "end", s, g, final[:, g, :], s_sum["end"], t * (S * G) + s * G + g + 1)

            def end_norm(t, s):
                for g in range(G):
                    normalize(t, "end", s, g, final[:, g, :])

            def slot(t, n, ff=True, before=True, after=True):
                has_m = (ff and n + 1 < SLOTS) or (n + 1 == SLOTS and after)
                mt, m = (t, n + 1) if n + 1 < SLOTS else (t + 1, 0)
                pt, pn = (t, n - 1) if n else (t - 1, SLOTS - 1)
                ends = ff and before and pn >= SLOTS - S
                late, sd_at = late_stream(t, n, ff, after), SD_AT + (n == 0)
                for f in range(FT):
                    if has_m and f == PROBS_AT + 1:
                        probsT_lo(mt, m)
                    if ff:
                        gelu_parts(t, n, f)
                    if f == 0 and ff and before:
                        feed_forward_norm(pt, pn)
                    if not ff and f in WEIGHTS_AT:
                        weights_lo(2 * n + WEIGHTS_AT.index(f))
                    if f < LATE and late:
                        heads_step(*late, SPAN + f)
                        if f == LATE - 1:
                            heads_stats(*late)
                    if f == LATE and late:
                        heads_norm(*late)
                    if has_m:
                        if f in (sd_at - 1, sd_at):
                            for g in range(2 * (f - sd_at + 1), 2 * (f - sd_at + 2)):
                                src_dst(mt, m, g)
                        if f == sd_at + 1:
                            sdT_lo(mt, m)
                        if f == sd_at + 2:
                            exponents(mt, m)
                            xa_parts(mt, m)
                        if f == SUM_AT + 1:
                            attention_sums(mt, m, range(0, 2))
                            attention_sums(mt, m, range(2, G))
                    if after:
                        heads_step(t + 1, n // 3, n % 3 * FT + f)
                    if ends and END_AT <= f < END_AT + G:
                        end_sum(pt, pn - (SLOTS - S), f - END_AT)
                        if f == END_AT + G - 1:
                            mean_var(pt, "end", pn - (SLOTS - S))
                if has_m:
                    mean_var(mt, "n1", m)
                if ff:
                    for g in range(0, 2):
                        feed_forward_sum(t, n, g)
                if has_m:
                    attention_norm(mt, m)
                if ff:
                    for g in range(2, G):
                        feed_forward_sum(t, n, g)
                if has_m:
                    nT_lo_parts(mt, m)
                if ff:
                    feed_forward_stats(t, n)
                if ends:
                    end_norm(pt, pn - (SLOTS - S))

            for n in range(SLOTS):
                slot(-1, n, ff=False, before=False)
            prep(dve.tensor_tensor(bias1_part[:, :], U0[:, 0:NB], cols[:, 0:NB], ALU.add))
            dve.tensor_tensor(bias1[:, :], U1[:, 0:NB], bias1_part[:, :], ALU.add).then_inc(s_bias, 1)
            slot(0, 0, before=False)
            with dve.Fori(0, TURNS - 2) as it:
                for n in range(1, SLOTS):
                    slot(it, n)
                slot(it + 1, 0)
            for n in range(1, SLOTS):
                slot(TURNS - 2, n)
            for n in range(SLOTS):
                slot(TURNS - 1, n, after=False)
            feed_forward_norm(TURNS - 1, SLOTS - 1)
            for g in range(G):
                end_sum(TURNS - 1, S - 1, g)
            mean_var(TURNS - 1, "end", S - 1)
            end_norm(TURNS - 1, S - 1)


_INS = ['x', 'adj', 'L0_gnn_W_proj', 'L0_gnn_W_att', 'L0_gnn_b_att', 'L1_gnn_attn_w', 'L1_gnn_attn_b',
        'L1_gnn_W1', 'L1_gnn_b1', 'L1_gnn_W2', 'L1_gnn_b2', 'L1_gnn_g1', 'L1_gnn_beta1', 'L1_gnn_g2',
        'L1_gnn_beta2']
_OUTS = [((64, 128, 256), 'float32')]


def kernel(**inputs):
    import numpy as _np
    import concourse.bacc as _bacc
    from concourse import mybir as _mybir
    from concourse.bass_utils import run_bass_kernel_spmd as _run

    nc = _bacc.Bacc("TRN2", target_bir_lowering=False, num_devices=1)
    arrays, args = {}, []
    for name in _INS:
        a = _np.ascontiguousarray(inputs[name])
        arrays[f"in_{name}_dram"] = a
        args.append(nc.dram_tensor(f"in_{name}_dram", a.shape, _mybir.dt.from_np(a.dtype),
                                   kind="ExternalInput").ap())
    for i, (shape, dtype) in enumerate(_OUTS):
        dt = _mybir.dt.from_np(_np.dtype(dtype))
        args.append(nc.dram_tensor(f"out_{i}_dram", shape, dt, kind="ExternalOutput").ap())
    graph_network(nc, *args)
    r = _run(nc, [arrays], core_ids=[0])
    return r.results[0]["out_0_dram"]
```
